# Optimizing a Trainium2 kernel written in Bass

```python
import numpy as np
import jax
import jax.numpy as jnp

def _softmax(x, axis=-1):
    return jax.nn.softmax(x, axis=axis)

def _gelu(x):
    return jax.nn.gelu(x, approximate=True)

def _silu(x):
    return jax.nn.silu(x)

def _sigmoid(x):
    return jax.nn.sigmoid(x)

def _layernorm(x, axis=-1, eps=1e-05):
    m = jnp.mean(x, axis=axis, keepdims=True)
    v = jnp.var(x, axis=axis, keepdims=True)
    return (x - m) / jnp.sqrt(v + eps)

def _scatter_add(tgt, idx, src, axis=0):
    return tgt.at[idx].add(src)

def _segment_sum(src, seg, n):
    return jax.ops.segment_sum(src, seg, n)
kernel_name = 'mk_adaln_d1_jaxref_r8_da1fba'

def setup_inputs(seed: int=0):
    np.random.seed(seed)
    _w = jnp.asarray

    def _L0_attn_setup():
        import jax, jax.numpy as jnp
        import numpy as np
        DIM = 128
        N_QUAT = DIM // 4
        LN_EPS = 1e-05
        NORM_EPS = 1e-12

        def quat_mul(q1, q2):
            r1, i1, j1, k1 = (q1[..., 0], q1[..., 1], q1[..., 2], q1[..., 3])
            r2, i2, j2, k2 = (q2[..., 0], q2[..., 1], q2[..., 2], q2[..., 3])
            r = r1 * r2 - i1 * i2 - j1 * j2 - k1 * k2
            i = r1 * i2 + i1 * r2 + j1 * k2 - k1 * j2
            j = r1 * j2 - i1 * k2 + j1 * r2 + k1 * i2
            k = r1 * k2 + i1 * j2 - j1 * i2 + k1 * r2
            return jnp.stack([r, i, j, k], axis=-1)

        def quat_conj(q):
            return q * jnp.array([1.0, -1.0, -1.0, -1.0], dtype=q.dtype)
        key = jax.random.key(seed)
        ks = jax.random.split(key, 7)
        B, L, D = (4, 512, DIM)
        s = 1.0 / np.sqrt(D)
        return {'x': jax.random.normal(ks[0], (B, L, D), dtype=jnp.float32), 'Wk': jax.random.normal(ks[1], (D, D), dtype=jnp.float32) * s, 'bk': jnp.zeros((D,), dtype=jnp.float32), 'Wv': jax.random.normal(ks[2], (D, D), dtype=jnp.float32) * s, 'bv': jnp.zeros((D,), dtype=jnp.float32), 'ln_g': jnp.ones((D,), dtype=jnp.float32), 'ln_b': jnp.zeros((D,), dtype=jnp.float32), 'Wo': jax.random.normal(ks[3], (D, D), dtype=jnp.float32) * s, 'bo': jnp.zeros((D,), dtype=jnp.float32)}
    _L0_attn_in = _L0_attn_setup()

    def _L0_ffn_setup():
        import jax, jax.numpy as jnp
        import numpy as np
        DIM = 128
        DEPTH = 6
        HEADS = 16
        DIM_HEAD = 64
        WINDOW = 32
        INNER = HEADS * DIM_HEAD
        DIM_INNER = int(DIM * 4 * 2 / 3)
        QK_SCALE = 8.0

        def shift_tokens(t):
            a, s = jnp.split(t, 2, -1)
            s = jnp.pad(s, ((0, 0), (1, 0), (0, 0)))[:, :-1]
            return jnp.concatenate([a, s], -1)

        def l2norm(t):
            return t / jnp.maximum(jnp.linalg.norm(t, axis=-1, keepdims=True), 1e-12)

        def rotate_half(x):
            x1, x2 = jnp.split(x, 2, -1)
            return jnp.concatenate([-x2, x1], -1)

        def rotary_tables(n):
            half = jnp.arange(0, DIM_HEAD, 2, dtype=jnp.float32)
            inv_freq = 1.0 / 10000.0 ** (half / DIM_HEAD)
            t = jnp.arange(n, dtype=jnp.float32)
            freqs = t[:, None] * inv_freq[None, :]
            freqs = jnp.concatenate([freqs, freqs], -1)
            base_scale = (half + 0.4 * DIM_HEAD) / (1.4 * DIM_HEAD)
            power = (t - n // 2) / (WINDOW // 2)
            scale = base_scale[None, :] ** power[:, None]
            scale = jnp.concatenate([scale, scale], -1)
            return (freqs, scale)

        def local_attention(q, k, v):
            b, h, n, d = q.shape
            w = WINDOW
            nw = n // w
            bq = q.reshape(b, h, nw, w, d)
            bk = k.reshape(b, h, nw, w, d)
            bv = v.reshape(b, h, nw, w, d)

            def look(t):
                p = jnp.pad(t, ((0, 0), (0, 0), (1, 0), (0, 0), (0, 0)))
                return jnp.concatenate([p[:, :, :nw], p[:, :, 1:]], axis=3)
            bk2, bv2 = (look(bk), look(bv))
            seq = jnp.arange(n).reshape(nw, w)
            seq_p = jnp.pad(seq, ((1, 0), (0, 0)), constant_values=-1)
            jt = jnp.concatenate([seq_p[:nw], seq_p[1:]], axis=1)
            it = seq[:, :, None]
            jb = jt[:, None, :]
            mask = (it < jb) | (it > jb + w) | (jb == -1)
            sim = jnp.einsum('bhwie,bhwje->bhwij', bq, bk2) * QK_SCALE
            sim = jnp.where(mask, -jnp.finfo(sim.dtype).max, sim)
            attn = jax.nn.softmax(sim, -1)
            out = jnp.einsum('bhwij,bhwje->bhwie', attn, bv2)
            return out.reshape(b, h, n, d)

        def attn_layer(x, Wqkv, qs, ksc, Wo):
            b, n, _ = x.shape
            qkv = x @ Wqkv
            q, k, v = jnp.split(qkv, 3, -1)
            sh = lambda t: t.reshape(b, n, HEADS, DIM_HEAD).transpose(0, 2, 1, 3)
            q, k, v = (sh(q), sh(k), sh(v))
            q = l2norm(q) * qs
            k = l2norm(k) * ksc
            freqs, scale = rotary_tables(n)
            cos, sin = (jnp.cos(freqs), jnp.sin(freqs))
            q = q * cos * scale + rotate_half(q) * sin * scale
            inv = 1.0 / scale
            k = k * cos * inv + rotate_half(k) * sin * inv
            out = local_attention(q, k, v)
            out = out.transpose(0, 2, 1, 3).reshape(b, n, INNER)
            return out @ Wo

        def ffn_layer(x, g, bln, W1, b1, W2, b2):
            mu = x.mean(-1, keepdims=True)
            var = ((x - mu) ** 2).mean(-1, keepdims=True)
            xn = (x - mu) / jnp.sqrt(var + 1e-05) * g + bln
            hg = xn @ W1 + b1
            a, gate = jnp.split(hg, 2, -1)
            return a * jax.nn.gelu(gate, approximate=False) @ W2 + b2
        key = jax.random.key(seed)
        ks = jax.random.split(key, 8)
        B, N = (2, 256)
        init = lambda k, shape: jax.random.normal(k, shape, jnp.float32) * 0.02
        return {'x': jax.random.normal(ks[0], (B, N, DIM), jnp.float32), 'Wqkv': init(ks[1], (DEPTH, DIM, 3 * INNER)), 'q_scale': jnp.ones((DEPTH, DIM_HEAD), jnp.float32), 'k_scale': jnp.ones((DEPTH, DIM_HEAD), jnp.float32), 'Wo': init(ks[2], (DEPTH, INNER, DIM)), 'ln_g': jnp.ones((DEPTH, DIM), jnp.float32), 'ln_b': jnp.zeros((DEPTH, DIM), jnp.float32), 'W1': init(ks[3], (DEPTH, DIM, 2 * DIM_INNER)), 'b1': jnp.zeros((DEPTH, 2 * DIM_INNER), jnp.float32), 'W2': init(ks[4], (DEPTH, DIM_INNER, DIM)), 'b2': jnp.zeros((DEPTH, DIM), jnp.float32)}
    _L0_ffn_in = _L0_ffn_setup()
    _L0_c = _w((lambda *s: np.random.randn(*s).astype(np.float32) * 0.05)(1, 128))
    _L0_wmod = _w((lambda *s: np.random.randn(*s).astype(np.float32) * 0.05)(128, 6 * 128) * 128 ** (-0.5))
    _d = {'L0_attn_x': _L0_attn_in['x'], 'L0_attn_Wk': _L0_attn_in['Wk'], 'L0_attn_bk': _L0_attn_in['bk'], 'L0_attn_Wv': _L0_attn_in['Wv'], 'L0_attn_bv': _L0_attn_in['bv'], 'L0_attn_ln_g': _L0_attn_in['ln_g'], 'L0_attn_ln_b': _L0_attn_in['ln_b'], 'L0_attn_Wo': _L0_attn_in['Wo'], 'L0_attn_bo': _L0_attn_in['bo'], 'L0_ffn_Wqkv': _L0_ffn_in['Wqkv'], 'L0_ffn_q_scale': _L0_ffn_in['q_scale'], 'L0_ffn_k_scale': _L0_ffn_in['k_scale'], 'L0_ffn_Wo': _L0_ffn_in['Wo'], 'L0_ffn_ln_g': _L0_ffn_in['ln_g'], 'L0_ffn_ln_b': _L0_ffn_in['ln_b'], 'L0_ffn_W1': _L0_ffn_in['W1'], 'L0_ffn_b1': _L0_ffn_in['b1'], 'L0_ffn_W2': _L0_ffn_in['W2'], 'L0_ffn_b2': _L0_ffn_in['b2'], 'L0_c': _L0_c, 'L0_wmod': _L0_wmod}
    _x0 = _d['L0_attn_x']
    _d['L0_attn_x'] = jax.random.normal(jax.random.fold_in(jax.random.key(seed), 1), (1, 2048, 128), dtype=_x0.dtype)
    del _x0
    return _d

def reference(L0_attn_x, L0_attn_Wk, L0_attn_bk, L0_attn_Wv, L0_attn_bv, L0_attn_ln_g, L0_attn_ln_b, L0_attn_Wo, L0_attn_bo, L0_ffn_Wqkv, L0_ffn_q_scale, L0_ffn_k_scale, L0_ffn_Wo, L0_ffn_ln_g, L0_ffn_ln_b, L0_ffn_W1, L0_ffn_b1, L0_ffn_W2, L0_ffn_b2, L0_c, L0_wmod):

    def _L0_attn_ref(x, Wk, bk, Wv, bv, ln_g, ln_b, Wo, bo):
        import jax, jax.numpy as jnp
        import numpy as np
        DIM = 128
        N_QUAT = DIM // 4
        LN_EPS = 1e-05
        NORM_EPS = 1e-12

        def quat_mul(q1, q2):
            r1, i1, j1, k1 = (q1[..., 0], q1[..., 1], q1[..., 2], q1[..., 3])
            r2, i2, j2, k2 = (q2[..., 0], q2[..., 1], q2[..., 2], q2[..., 3])
            r = r1 * r2 - i1 * i2 - j1 * j2 - k1 * k2
            i = r1 * i2 + i1 * r2 + j1 * k2 - k1 * j2
            j = r1 * j2 - i1 * k2 + j1 * r2 + k1 * i2
            k = r1 * k2 + i1 * j2 - j1 * i2 + k1 * r2
            return jnp.stack([r, i, j, k], axis=-1)

        def quat_conj(q):
            return q * jnp.array([1.0, -1.0, -1.0, -1.0], dtype=q.dtype)
        B, L, D = x.shape
        keys = (x @ Wk.T + bk).reshape(B, L, N_QUAT, 4)
        knorm = jnp.linalg.norm(keys, axis=-1, keepdims=True)
        keys = keys / jnp.maximum(knorm, NORM_EPS)
        values = (x @ Wv.T + bv).reshape(B, L, N_QUAT, 4)
        bound = quat_mul(values, keys)
        memory = jnp.cumsum(bound, axis=1)
        retrieved = quat_mul(memory, quat_conj(keys)).reshape(B, L, D)
        positions = jnp.arange(1, L + 1, dtype=x.dtype)
        retrieved = retrieved / jnp.sqrt(positions)[None, :, None]
        mu = jnp.mean(retrieved, axis=-1, keepdims=True)
        var = jnp.var(retrieved, axis=-1, keepdims=True)
        normed = (retrieved - mu) / jnp.sqrt(var + LN_EPS) * ln_g + ln_b
        return x + (normed @ Wo.T + bo)

    def _L0_ffn_ref(x, Wqkv, q_scale, k_scale, Wo, ln_g, ln_b, W1, b1, W2, b2):
        import jax, jax.numpy as jnp
        import numpy as np
        DIM = 128
        DEPTH = 6
        HEADS = 16
        DIM_HEAD = 64
        WINDOW = 32
        INNER = HEADS * DIM_HEAD
        DIM_INNER = int(DIM * 4 * 2 / 3)
        QK_SCALE = 8.0

        def shift_tokens(t):
            a, s = jnp.split(t, 2, -1)
            s = jnp.pad(s, ((0, 0), (1, 0), (0, 0)))[:, :-1]
            return jnp.concatenate([a, s], -1)

        def l2norm(t):
            return t / jnp.maximum(jnp.linalg.norm(t, axis=-1, keepdims=True), 1e-12)

        def rotate_half(x):
            x1, x2 = jnp.split(x, 2, -1)
            return jnp.concatenate([-x2, x1], -1)

        def rotary_tables(n):
            half = jnp.arange(0, DIM_HEAD, 2, dtype=jnp.float32)
            inv_freq = 1.0 / 10000.0 ** (half / DIM_HEAD)
            t = jnp.arange(n, dtype=jnp.float32)
            freqs = t[:, None] * inv_freq[None, :]
            freqs = jnp.concatenate([freqs, freqs], -1)
            base_scale = (half + 0.4 * DIM_HEAD) / (1.4 * DIM_HEAD)
            power = (t - n // 2) / (WINDOW // 2)
            scale = base_scale[None, :] ** power[:, None]
            scale = jnp.concatenate([scale, scale], -1)
            return (freqs, scale)

        def local_attention(q, k, v):
            b, h, n, d = q.shape
            w = WINDOW
            nw = n // w
            bq = q.reshape(b, h, nw, w, d)
            bk = k.reshape(b, h, nw, w, d)
            bv = v.reshape(b, h, nw, w, d)

            def look(t):
                p = jnp.pad(t, ((0, 0), (0, 0), (1, 0), (0, 0), (0, 0)))
                return jnp.concatenate([p[:, :, :nw], p[:, :, 1:]], axis=3)
            bk2, bv2 = (look(bk), look(bv))
            seq = jnp.arange(n).reshape(nw, w)
            seq_p = jnp.pad(seq, ((1, 0), (0, 0)), constant_values=-1)
            jt = jnp.concatenate([seq_p[:nw], seq_p[1:]], axis=1)
            it = seq[:, :, None]
            jb = jt[:, None, :]
            mask = (it < jb) | (it > jb + w) | (jb == -1)
            sim = jnp.einsum('bhwie,bhwje->bhwij', bq, bk2) * QK_SCALE
            sim = jnp.where(mask, -jnp.finfo(sim.dtype).max, sim)
            attn = jax.nn.softmax(sim, -1)
            out = jnp.einsum('bhwij,bhwje->bhwie', attn, bv2)
            return out.reshape(b, h, n, d)

        def attn_layer(x, Wqkv, qs, ksc, Wo):
            b, n, _ = x.shape
            qkv = x @ Wqkv
            q, k, v = jnp.split(qkv, 3, -1)
            sh = lambda t: t.reshape(b, n, HEADS, DIM_HEAD).transpose(0, 2, 1, 3)
            q, k, v = (sh(q), sh(k), sh(v))
            q = l2norm(q) * qs
            k = l2norm(k) * ksc
            freqs, scale = rotary_tables(n)
            cos, sin = (jnp.cos(freqs), jnp.sin(freqs))
            q = q * cos * scale + rotate_half(q) * sin * scale
            inv = 1.0 / scale
            k = k * cos * inv + rotate_half(k) * sin * inv
            out = local_attention(q, k, v)
            out = out.transpose(0, 2, 1, 3).reshape(b, n, INNER)
            return out @ Wo

        def ffn_layer(x, g, bln, W1, b1, W2, b2):
            mu = x.mean(-1, keepdims=True)
            var = ((x - mu) ** 2).mean(-1, keepdims=True)
            xn = (x - mu) / jnp.sqrt(var + 1e-05) * g + bln
            hg = xn @ W1 + b1
            a, gate = jnp.split(hg, 2, -1)
            return a * jax.nn.gelu(gate, approximate=False) @ W2 + b2
        for i in range(DEPTH):
            x = attn_layer(shift_tokens(x), Wqkv[i], q_scale[i], k_scale[i], Wo[i]) + x
            x = ffn_layer(shift_tokens(x), ln_g[i], ln_b[i], W1[i], b1[i], W2[i], b2[i]) + x
        return x
    x = L0_attn_x
    mod = (_silu(L0_c) @ L0_wmod).reshape(L0_c.shape[0], 6, 1, -1)
    sa, ca, ga, sb, cb, gb = (mod[:, 0], mod[:, 1], mod[:, 2], mod[:, 3], mod[:, 4], mod[:, 5])
    ga = (2 * (ga >= 0) - 1) * jnp.maximum(jnp.abs(ga), 0.25)
    gb = (2 * (gb >= 0) - 1) * jnp.maximum(jnp.abs(gb), 0.25)
    h = _layernorm(x, axis=-1) * (1 + ca) + sa
    x = x + ga * _L0_attn_ref(h, L0_attn_Wk, L0_attn_bk, L0_attn_Wv, L0_attn_bv, L0_attn_ln_g, L0_attn_ln_b, L0_attn_Wo, L0_attn_bo)
    h = _layernorm(x, axis=-1) * (1 + cb) + sb
    x = x + gb * _L0_ffn_ref(h, L0_ffn_Wqkv, L0_ffn_q_scale, L0_ffn_k_scale, L0_ffn_Wo, L0_ffn_ln_g, L0_ffn_ln_b, L0_ffn_W1, L0_ffn_b1, L0_ffn_W2, L0_ffn_b2)
    return x

_drawn_inputs = setup_inputs


def setup_inputs(seed=0):
    import zlib

    import numpy as np

    out = dict(_drawn_inputs(seed))
    spreads = {'L0_attn_bk': (0.0, 0.1),
     'L0_attn_bv': (0.0, 0.339),
     'L0_attn_ln_g': (1.0, 0.2),
     'L0_attn_ln_b': (0.0, 0.321),
     'L0_attn_bo': (0.0, 0.355),
     'L0_ffn_q_scale': (1.0, 0.6),
     'L0_ffn_k_scale': (1.0, 0.6),
     'L0_ffn_ln_g': (1.0, 0.6),
     'L0_ffn_ln_b': (0.0, 0.8),
     'L0_ffn_b1': (0.0, 0.8),
     'L0_ffn_b2': (0.0, 0.642)}
    factors = {'L0_ffn_W1': 7.612, 'L0_ffn_W2': 7.484}
    for name, (base, spread) in spreads.items():
        noise = np.random.default_rng([zlib.crc32(name.encode()), seed]).standard_normal(out[name].shape)
        drawn = base * np.exp(spread * noise) if base else spread * noise
        out[name] = jnp.asarray(drawn.astype(out[name].dtype))
    for name, factor in factors.items():
        out[name] = (out[name] * factor).astype(out[name].dtype)
    return out
```

```python
import numpy as np
import concourse.bass as bass
from concourse import mybir
from contextlib import ExitStack

F32 = mybir.dt.float32
BF16 = mybir.dt.bfloat16
I32 = mybir.dt.int32
ALU = mybir.AluOpType
ACT = mybir.ActivationFunctionType
AX = mybir.AxisListType.X

N, D = 2048, 128
P = 128
NT = N // P
LAYERS, H, DH, W = 6, 16, 64, 32
HP = H // 2
NW = P // W
INNER = H * DH
DI = 341
CH = 512
NC_ = N // CH
NQ = N * D // (P * 4)
KT = [128, 128, DI - 256]
LN_EPS = 1e-5
NORM_GUARD = 1e-24
MASKED = -1e30
RSQRT_MAGIC = 0x5F3759DF

C_ID, C_TRI, C_ONE, C_AVG, C_CEN, C_MASK, C_MASK0 = 0, 128, 256, 384, 512, 640, 704
C_KS, C_RSQ, C_EPS, C_END = 768, 769, 785, 786
R_BKV, R_G, R_B, R_BO, R_END = 0, 256, 384, 512, 640
L_G, L_B, L_B2, L_BA, L_BG, L_END = 0, 1, 2, 3, 6, 9

GATE_BANK, A_BANK = [0, 1, 2], [3, 4, 5]
AD_SILU, AD_MOD, AD_XC1, AD_H, AD_KV, AD_PRE, AD_XC2, AD_N, AD_XC3, AD_H2, C_OUT = 4, 18, 21, 40, 43, 103, 135, 154, 161, 180, 182
AA_EXPC, AA_SQ1, AA_HT, AA_KSQ, AA_MEM, AA_SQ2, AA_NT, AA_SQ3, A_XT = range(1, 10)
A_MOD, A_T1, A_KV, A_CUM, A_T2, A_WO, A_T3, C_T = range(1, 9)
FREE = 1
NEWTON = 4
NORM_LINKS = 1 + 2 + 3 * NEWTON

PERM = [[0, 1, 2, 3], [1, 0, 3, 2], [2, 3, 0, 1], [3, 2, 1, 0]]
SIGN = [[1, 1, 1, 1], [-1, 1, -1, 1], [-1, 1, 1, -1], [-1, -1, 1, 1]]


def program(nc, x_d, cst_d, row_d, c_d, wmod_d, wkv_d, woa_d, tab_d, scl_d, wqkv_d, wo_d, w1_d, w2_d, prm_d,
            out_d):
    ctx = ExitStack()
    with ctx:
        def sb(name, shape, dt=F32):
            return ctx.enter_context(nc.sbuf_tensor(name, shape, dt))

        def sem(name):
            return ctx.enter_context(nc.semaphore(name))

        cst = sb("cst", [P, C_END])
        row = sb("row", [P, R_END])
        maskb = sb("maskb", [P, 2, 8, 2 * W], BF16)
        identb = sb("identb", [P, P], BF16)
        mod = sb("mod", [P, 6 * D])
        x1 = sb("x1", [P, NT, D])
        xT = sb("xT", [P, 1 + N])
        wbuf = sb("wbuf", [P, 3 * INNER])
        wo = sb("wo", [P, HP, D])
        w1 = sb("w1", [P, 2 * DI])
        w2 = sb("w2", [P, 3, D])
        prm = sb("prm", [P, LAYERS, L_END])
        pl = sb("pl", [P, L_END])
        scl = sb("scl", [P, LAYERS, 4 * DH])
        tab = sb("tab", [P, NT, 4 * DH])
        tabl = sb("tabl", [P, NT, 4 * DH])
        xs = sb("xs", [P, P])
        sq = sb("sq", [P, 2 * INNER])
        t1 = sb("t1", [P, 2 * INNER])
        t2 = sb("t2", [P, 2 * INNER])
        u = sb("u", [P, 2 * INNER])
        ss = sb("ss", [P, 2 * H])
        rn = sb("rn", [P, 2 * H])
        ra = sb("ra", [P, 2 * H])
        vs = sb("vs", [P, 2, HP * DH])
        vf = sb("vf", [P, 2, NW, HP * DH])
        qT = sb("qT", [P, HP, P])
        kT = sb("kT", [P, 2, HP, W + P])
        pr = sb("pr", [P, H, 2 * W])
        mx = sb("mx", [P, H])
        rs = sb("rs", [P, H])
        ri = sb("ri", [P, H])
        pT = sb("pT", [P, HP, P])
        od = sb("od", [P, 2 * INNER])
        o = od[:, 0:INNER]
        oT = od[:, INNER:2 * INNER].rearrange("p (k n) -> p k n", n=P)
        st = sb("st", [P, 512])
        st2 = sb("st2", [P, 512])
        st3 = sb("st3", [P, 512])
        tok = lambda b: b[:, 0:N].rearrange("p (t d) -> p t d", d=D)
        h_keep = od[:, :]
        pre = xT[:, 1:1 + N].rearrange("p (t d) -> p t d", d=D)
        ps = ctx.enter_context(nc.psum_tensor("ps", [P, 8, 512], F32))

        v_scr = nc.dram_tensor("v_scratch", [W + N, 2 * HP * DH], F32, kind="Internal").ap()

        in_x, in_cst, in_vec, in_wa = sem("in_x"), sem("in_cst"), sem("in_vec"), sem("in_wa")
        in_tab, in_prm, zero_row = sem("in_tab"), sem("in_prm"), sem("zero_row")
        in_wqkv, in_wo, in_w12 = sem("in_wqkv"), sem("in_wo"), sem("in_w12")
        cleared, tabs_ready, masks_ready = sem("cleared"), sem("tabs_ready"), sem("masks_ready")
        a_dve, a_act, a_pe = sem("a_dve"), sem("a_act"), sem("a_pe")
        xs_ready, proj_done, v_evac = sem("xs_ready"), sem("proj_done"), sem("v_evac")
        v_stored, v_frames = sem("v_stored"), sem("v_frames")
        squared, rotated, added, inv_norm, link = sem("squared"), sem("rotated"), sem("added"), sem("inv_norm"), sem("link")
        q_normed, k_normed, q_trans, k_trans = sem("q_normed"), sem("k_normed"), sem("q_trans"), sem("k_trans")
        q_evac, k_evac, k_carried = sem("q_evac"), sem("k_evac"), sem("k_carried")
        scored, max_ready, shifted, exp_done = sem("scored"), sem("max_ready"), sem("shifted"), sem("exp_done")
        sum_ready, rsum_ready = sem("sum_ready"), sem("rsum_ready")
        p_trans, p_evac, av_done, o_normed = sem("p_trans"), sem("p_evac"), sem("av_done"), sem("o_normed")
        o_trans, o_evac, y_done, x_added = sem("o_trans"), sem("o_evac"), sem("y_done"), sem("x_added")
        f_xs, f_cen, f_sq, f_var, f_cp = sem("f_xs"), sem("f_cen"), sem("f_sq"), sem("f_var"), sem("f_cp")
        f_std, f_rstd, f_xn, f_aff, f_prm = sem("f_std"), sem("f_rstd"), sem("f_xn"), sem("f_aff"), sem("f_prm")
        f_gate, f_a, f_gelu, f_ag, f_y, f_x = sem("f_gate"), sem("f_a"), sem("f_gelu"), sem("f_ag"), sem("f_y"), sem("f_x")
        out_done = sem("out_done")

        ident = cst[:, C_ID:C_ID + P]
        block = ctx.enter_context(nc.Block())

        fxs = sq[:, 0:N].rearrange("p (c n) -> p c n", n=CH)
        fsq = t1[:, 0:N].rearrange("p (c n) -> p c n", n=CH)
        fxc = t2[:, 0:N].rearrange("p (c n) -> p c n", n=CH)
        fg = u[:, 0:3 * CH].rearrange("p (k n) -> p k n", n=CH)
        avg = cst[:, C_AVG:C_AVG + P]
        cen = cst[:, C_CEN:C_CEN + P]

        @block.sync
        def _(sp):
            for s in (v_frames, av_done, y_done, proj_done, k_trans, scored, rotated, v_stored, inv_norm,
                      f_ag, f_y, shifted, x_added, o_normed, added, p_trans, o_trans, f_x):
                sp.sem_inc(s, FREE)
            sp.dma_start(x1[:, :, :], x_d.rearrange("(t p) d -> p t d", p=P)).then_inc(in_x, 16)
            sp.dma_start(cst[:, :], cst_d).then_inc(in_cst, 16)
            sp.dma_start(st[:, 0:1], c_d).then_inc(in_vec, 16)
            sp.dma_start(wo[:, 0:6, :], wmod_d.rearrange("p (a d) -> p a d", d=D)).then_inc(in_vec, 16)
            sp.dma_start(row[:, :], row_d.partition_broadcast(P)).then_inc(in_vec, 16)
            sp.dma_start(w1[:, 0:256], wkv_d).then_inc(in_wa, 16)
            sp.dma_start(w1[:, 256:384], woa_d).then_inc(in_wa, 16)
            sp.dma_start(scl[:, :, :], scl_d.partition_broadcast(P)).then_inc(in_tab, 16)
            sp.dma_start(tab[:, :, :], tab_d.rearrange("(t p) c -> p t c", p=P)).then_inc(in_tab, 16)
            sp.dma_start(prm[:, :, :], prm_d).then_inc(in_prm, 16)
            sp.wait_ge(cleared, 1)
            sp.dma_start(v_scr[0:W, :], vf[0:W, 0, 0:2, :].rearrange("p w n -> p (w n)")).then_inc(zero_row, 16)
            sp.wait_ge(zero_row, 16)
            sp.wait_ge(a_pe, A_MOD)
            with sp.Fori(0, LAYERS) as L:
                rows, n_proj, n_y, n_xs = (sp.snap(x) for x in (L * P, L * (6 * NT) + FREE, L * NT + FREE, L * (2 * NT) + 2))
                sp.wait_ge(proj_done, n_proj)
                sp.dma_start(wbuf[:, :], wqkv_d[bass.ds(rows, P), :]).then_inc(in_wqkv, 16)
                sp.wait_ge(y_done, n_y)
                sp.dma_start(wo[:, :, :], wo_d[bass.ds(rows, P), :].rearrange("p (k d) -> p k d", d=D)).then_inc(in_wo, 16)
                sp.wait_ge(xs_ready, n_xs)
                sp.dma_start(w1[:, :], w1_d[bass.ds(rows, P), :]).then_inc(in_w12, 16)
                sp.dma_start(w2[:, :, :], w2_d[bass.ds(rows, P), :].rearrange("p (k d) -> p k d", d=D)).then_inc(in_w12, 16)
                with sp.Fori(0, NT) as t:
                    g = L * NT + t
                    even, odd, n_v, n_fr, n_st, n_av = (sp.snap(x) for x in (t * P, t * P + W, g * 2 + 2, g * 64 + FREE, g * 16 + 16 + FREE, g + FREE))
                    sp.wait_ge(av_done, n_av)
                    sp.wait_ge(v_frames, n_fr)
                    sp.wait_ge(v_evac, n_v)
                    sp.dma_start(v_scr[bass.ds(odd, P), :], vs[:, :, :].rearrange("p a n -> p (a n)")).then_inc(v_stored, 16)
                    sp.wait_ge(v_stored, n_st)
                    for a in range(2):
                        for w, first in enumerate((even, odd)):
                            src = v_scr[bass.ds(first, P), a * HP * DH:(a + 1) * HP * DH]
                            sp.dma_start(vf[DH * a:DH * a + DH, a, w:NW:2, :],
                                         src.rearrange("(w p) n -> p w n", p=2 * W)).then_inc(v_frames, 16)
            sp.wait_ge(a_dve, C_OUT)
            sp.dma_start(out_d.rearrange("(t p) d -> p t d", p=P), x1[:, :, :]).then_inc(out_done, 16)
            sp.wait_ge(out_done, 16)
            sp.wait_ge(v_stored, LAYERS * NT * 16 + FREE)
            sp.wait_ge(v_frames, LAYERS * NT * 64 + FREE)

        @block.gpsimd
        def _(pool):
            pool.memset(vf[:, :, :, :], 0.0).then_inc(cleared, 1)
            pool.memset(kT[:, :, :, :], 0.0).then_inc(cleared, 1)
            pool.memset(xT[:, 0:1], 0.0).then_inc(cleared, 1)
            pool.wait_ge(in_cst, 16)
            pool.tensor_copy(identb[:, :], ident).then_inc(masks_ready, 1)
            for m, c in enumerate((C_MASK, C_MASK0)):
                pool.tensor_copy(maskb[:, m, :, :], cst[:, c:c + 2 * W].unsqueeze(1).broadcast_to([P, 8, 2 * W])).then_inc(masks_ready, 1)
            def add_and_carry(g):
                pool.wait_ge(k_trans, g * 2 + FREE)
                pool.wait_ge(scored, g + FREE)
                for c in range(4):
                    pool.wait_ge(rotated, g * 4 + c + 1 + FREE)
                    s = slice(c * 512, c * 512 + 512)
                    pool.tensor_tensor(u[:, s], t1[:, s], t2[:, s], ALU.add).then_inc(added, 1)
                pool.tensor_scalar(kT[:, :, :, 0:W], kT[:, :, :, P:P + W], cst[:, C_KS:C_KS + 1], 1.0,
                                   ALU.mult, ALU.mult).then_inc(k_carried, 1)

            pool.wait_ge(in_tab, 32)
            with pool.Fori(0, LAYERS) as L:
                pool.wait_ge(rotated, L * (4 * NT) + FREE)
                pool.tensor_tensor(tabl[:, :, :], tab[:, :, :],
                                   scl[:, bass.ds(L, 1), :].broadcast_to([P, NT, 4 * DH]), ALU.mult).then_inc(tabs_ready, 1)
                add_and_carry(L * NT)
                with pool.Fori(0, NT - 1) as t:
                    add_and_carry(L * NT + t + 1)

        @block.scalar
        def _(act):
            step = [0]

            def did(ins, sem_=a_act):
                step[0] += 1
                ins.then_inc(sem_, 1)
                return step[0]

            act.wait_ge(in_vec, 48)
            assert did(act.activation(st[:, 1:2], st[:, 0:1], ACT.Exp, scale=-1.0)) == AA_EXPC
            act.wait_ge(a_dve, AD_XC1)
            assert did(act.activation(tok(t2), tok(t1), ACT.Square)) == AA_SQ1
            act.wait_ge(a_pe, A_T1)
            assert did(act.activation(u[:, 0:N], ps[:, 0:4, :].rearrange("p b n -> p (b n)"), ACT.Copy)) == AA_HT
            act.wait_ge(a_dve, AD_KV)
            assert did(act.activation(sq[:, 0:N], t1[:, 0:N], ACT.Square)) == AA_KSQ
            act.wait_ge(a_pe, A_CUM)
            assert did(act.activation(t2[:, 0:N], ps[:, 0:4, :].rearrange("p b n -> p (b n)"), ACT.Copy)) == AA_MEM
            act.wait_ge(a_dve, AD_XC2)
            assert did(act.activation(tok(t2), tok(u), ACT.Square)) == AA_SQ2
            act.wait_ge(a_pe, A_T2)
            assert did(act.activation(t1[:, 0:N], ps[:, 4:8, :].rearrange("p b n -> p (b n)"), ACT.Copy)) == AA_NT
            act.wait_ge(a_dve, AD_XC3)
            assert did(act.activation(tok(t2), tok(t1), ACT.Square)) == AA_SQ3
            act.wait_ge(a_pe, A_T3)
            act.wait_ge(cleared, 3)
            assert did(act.activation(xT[:, 1:1 + N], ps[:, 4:8, :].rearrange("p b n -> p (b n)"), ACT.Copy)) == A_XT

            def evac_v(g):
                act.wait_ge(v_stored, g * 16 + FREE)
                for a in range(2):
                    act.wait_ge(proj_done, g * 6 + a + 1 + FREE)
                    act.activation(vs[:, a, :], ps[:, a, :], ACT.Copy).then_inc(v_evac, 1)

            def squares(g, chunks):
                act.wait_ge(inv_norm, g + FREE)
                for c in chunks:
                    act.wait_ge(proj_done, g * 6 + c + 3 + FREE)
                    act.activation(sq[:, c * 512:c * 512 + 512], ps[:, c % 2, :], ACT.Square).then_inc(squared, 1)

            def probabilities(g):
                act.wait_ge(shifted, g + 1 + FREE)
                act.activation(pr[:, :, :], pr[:, :, :], ACT.Exp, scale=8.0).then_inc(exp_done, 1)

            def evac_p(g):
                act.wait_ge(av_done, g + FREE)
                for b in range(2):
                    act.wait_ge(p_trans, g * 2 + b + 1 + FREE)
                    act.activation(pT[:, 4 * b:4 * b + 4, :], bank(2 + b), ACT.Copy).then_inc(p_evac, 1)

            def evac_qk(g):
                act.wait_ge(scored, g + FREE)
                for b in range(2):
                    act.wait_ge(q_trans, g * 2 + b + 1)
                    act.activation(qT[:, 4 * b:4 * b + 4, :], bank(2 + b), ACT.Copy).then_inc(q_evac, 1)
                act.wait_ge(k_carried, g + 1)
                for b in range(2):
                    act.wait_ge(k_trans, g * 2 + b + 1 + FREE)
                    for a in range(2):
                        r = slice(DH * a, DH * a + DH)
                        act.activation(kT[r, a, 4 * b:4 * b + 4, W:W + P], bank(2 + b)[r], ACT.Copy).then_inc(k_evac, 1)

            def evac_o(g):
                act.wait_ge(y_done, g + FREE)
                for b in range(2):
                    act.wait_ge(o_trans, g * 2 + b + 1 + FREE)
                    act.activation(oT[:, 4 * b:4 * b + 4, :], bank(2 + b), ACT.Copy).then_inc(o_evac, 1)

            def bank(b):
                return ps[:, b, :].rearrange("p (a n) -> p a n", n=P)

            with act.Fori(0, LAYERS) as L:
                evac_v(L * NT)
                squares(L * NT, range(4))
                evac_qk(L * NT)
                with act.Fori(0, NT - 1) as t:
                    g = L * NT + t
                    evac_v(g + 1)
                    squares(g + 1, (0, 1))
                    probabilities(g)
                    squares(g + 1, (2, 3))
                    evac_p(g)
                    evac_qk(g + 1)
                    evac_o(g)
                g = L * NT + (NT - 1)
                probabilities(g)
                evac_p(g)
                evac_o(g)
                def square(c):
                    act.wait_ge(f_cen, L * NC_ + c + 1)
                    act.activation(fsq[:, c, :], ps[:, c % 2, :], ACT.Square).then_inc(f_sq, 1)

                def deviation(c):
                    act.wait_ge(f_var, L * NC_ + c + 1)
                    act.activation(fsq[:, c, :], ps[:, 2 + c % 2, :], ACT.Sqrt, bias=cst[:, C_EPS:C_EPS + 1]).then_inc(f_std, 1)

                square(0)
                for c in range(NC_):
                    if c + 1 < NC_:
                        square(c + 1)
                    deviation(c)
                for c in range(NC_):
                    act.wait_ge(f_ag, L * (3 * NC_) + 3 * c + FREE)
                    act.wait_ge(f_y, L * NC_ + c + FREE)
                    for k in range(3):
                        act.wait_ge(f_gate, L * (3 * NC_) + 3 * c + k + 1)
                        act.activation(fg[0:KT[k], k, :], ps[0:KT[k], GATE_BANK[k], :], ACT.Gelu,
                                       bias=pl[0:KT[k], L_BG + k:L_BG + k + 1]).then_inc(f_gelu, 1)

        @block.tensor
        def _(pe):
            step = [0]

            def did(ins):
                step[0] += 1
                ins.then_inc(a_pe, 1)
                return step[0]

            def tile(b, t):
                return ps[:, b + t // 4, (t % 4) * P:(t % 4) * P + P]

            pe.wait_ge(a_dve, AD_SILU)
            for j in range(2):
                mm = pe.matmul(ps[:, 6 + j, 0:384], st2[:, 0:P], wo[:, 3 * j:3 * j + 3, :], start=True, stop=True)
            assert did(mm) == A_MOD
            pe.wait_ge(a_dve, AD_H)
            for t in range(NT):
                mm = pe.transpose(tile(0, t), tok(sq)[:, t, :], ident)
            assert did(mm) == A_T1
            pe.wait_ge(a_act, AA_HT)
            pe.wait_ge(a_dve, AD_MOD)
            pe.wait_ge(in_wa, 32)
            for t in range(NT):
                mm = pe.matmul(ps[:, t // 2, (t % 2) * 256:(t % 2) * 256 + 256], u[:, t * P:t * P + P], w1[:, 0:256], start=True, stop=True)
            assert did(mm) == A_KV
            pe.wait_ge(a_dve, AD_PRE)
            for t in range(NT):
                mm = pe.matmul(tile(0, t), cst[:, C_TRI:C_TRI + P], tok(u)[:, t, :], start=True, stop=(t == 0))
                if t:
                    mm = pe.matmul(tile(0, t), cst[:, C_ONE:C_ONE + P], pre[:, t, :], start=False, stop=True)
            assert did(mm) == A_CUM
            pe.wait_ge(a_dve, AD_N)
            for t in range(NT):
                mm = pe.transpose(tile(4, t), tok(u)[:, t, :], ident)
            assert did(mm) == A_T2
            pe.wait_ge(a_act, AA_NT)
            for t in range(NT):
                mm = pe.matmul(tile(0, t), t1[:, t * P:t * P + P], w1[:, 256:384], start=True, stop=True)
            assert did(mm) == A_WO
            pe.wait_ge(a_dve, AD_H2)
            for t in range(NT):
                mm = pe.transpose(tile(4, t), tok(t1)[:, t, :], ident)
            assert did(mm) == A_T3

            def project(g):
                pe.wait_ge(xs_ready, g * 2 + 2)
                pe.wait_ge(rotated, g * 4 + FREE)
                for c, col in enumerate((4, 5, 0, 1, 2, 3)):
                    if 2 <= c < 4:
                        pe.wait_ge(v_evac, g * 2 + c - 1)
                    if c >= 4:
                        pe.wait_ge(rotated, g * 4 + c - 3 + FREE)
                    pe.matmul(ps[:, c % 2, :], xs[:, :], wbuf[:, col * 512:col * 512 + 512],
                              start=True, stop=True).then_inc(proj_done, 1)

            def transpose4(b, src, done):
                for j in range(4):
                    mm = pe.transpose(ps[:, 2 + b, j * P:j * P + P], src[:, (4 * b + j) * P:(4 * b + j + 1) * P], ident)
                mm.then_inc(done, 1)

            def transpose_qk(g):
                pe.wait_ge(q_normed, g + 1)
                transpose4(0, u[:, 0:INNER], q_trans)
                transpose4(1, u[:, 0:INNER], q_trans)
                pe.wait_ge(k_normed, g + 1)
                for b in range(2):
                    pe.wait_ge(q_evac, g * 2 + b + 1)
                    transpose4(b, u[:, INNER:2 * INNER], k_trans)

            def scores(g, m):
                pe.wait_ge(k_evac, g * 4 + 4)
                pe.wait_ge(q_evac, g * 2 + 2)
                pe.wait_ge(shifted, g + FREE)
                for b in range(2):
                    bk = ps[:, 4 + b, :]
                    pe.matmul(bk, identb[:, :], maskb[:, m, :, :].rearrange("p h n -> p (h n)"), start=True, stop=True)
                    for j in range(4):
                        hp = 4 * b + j
                        for w in range(NW):
                            last = pe.matmul(ps[W * w:W * w + W, 4 + b, j * P:j * P + P], qT[:, hp, W * w:W * w + W],
                                             kT[:, :, hp, W * w:W * w + 2 * W], start=False, stop=True,
                                             skip_group_check=True)
                last.then_inc(scored, 1)

            def transpose_p(g):
                pe.wait_ge(exp_done, g + 1)
                pe.wait_ge(x_added, g + FREE)
                pf = pr[:, :, :].rearrange("p h n -> p (h n)")
                transpose4(0, pf, p_trans)
                transpose4(1, pf, p_trans)

            def values(g):
                pe.wait_ge(v_frames, g * 64 + 64 + FREE)
                pe.wait_ge(p_evac, g * 2 + 2)
                pe.wait_ge(o_normed, g + FREE)
                for hp in range(HP):
                    for w in range(NW):
                        last = pe.matmul(ps[W * w:W * w + W, 6 + hp // 4, (hp % 4) * P:(hp % 4) * P + P],
                                         pT[:, hp, W * w:W * w + W], vf[:, :, w, hp * DH:hp * DH + DH],
                                         start=True, stop=True)
                last.then_inc(av_done, 1)

            def transpose_o(g, gk):
                pe.wait_ge(o_normed, g + 1 + FREE)
                for b in range(2):
                    pe.wait_ge(k_evac, gk * 4 - 2 + 2 * b)
                    transpose4(b, o, o_trans)

            def project_o(g):
                for k in range(HP):
                    pe.wait_ge(o_evac, g * 2 + 1 + k // 4)
                    mm = pe.matmul(ps[:, 2, 0:P], wo[:, k, :], oT[:, k, :], start=(k == 0), stop=(k == HP - 1))
                mm.then_inc(y_done, 1)

            pe.wait_ge(masks_ready, 3)
            with pe.Fori(0, LAYERS) as L:
                pe.wait_ge(in_wqkv, L * 16 + 16)
                pe.wait_ge(in_wo, L * 16 + 16)
                project(L * NT)
                transpose_qk(L * NT)
                scores(L * NT, 1)
                with pe.Fori(0, NT - 1) as t:
                    g = L * NT + t
                    project(g + 1)
                    transpose_p(g)
                    values(g)
                    transpose_qk(g + 1)
                    transpose_o(g, g + 2)
                    project_o(g)
                    scores(g + 1, 0)
                g = L * NT + (NT - 1)
                transpose_p(g)
                values(g)
                transpose_o(g, g + 1)
                project_o(g)
                def centre(c):
                    f = L * NC_ + c
                    pe.wait_ge(f_xs, f * 2 + 2)
                    if c >= 2:
                        pe.wait_ge(f_cp, f - 1)
                    pe.matmul(ps[:, c % 2, :], cen, fxs[:, c, :], start=True, stop=True).then_inc(f_cen, 1)

                def variance(c):
                    f = L * NC_ + c
                    pe.wait_ge(f_sq, f + 1)
                    if c >= 2:
                        pe.wait_ge(f_std, f - 1)
                    pe.matmul(ps[:, 2 + c % 2, :], avg, fsq[:, c, :], start=True, stop=True).then_inc(f_var, 1)

                centre(0)
                for c in range(NC_):
                    if c + 1 < NC_:
                        centre(c + 1)
                    variance(c)
                pe.wait_ge(f_cp, L * NC_ + NC_)
                pe.wait_ge(f_std, L * NC_ + NC_)
                pe.wait_ge(in_w12, L * 32 + 32)
                for c in range(NC_):
                    f = L * NC_ + c
                    pe.wait_ge(f_aff, f + 1)
                    for k in range(3):
                        if c:
                            pe.wait_ge(f_gelu, L * (3 * NC_) + 3 * c - 2 + k)
                        pe.matmul(ps[0:KT[k], GATE_BANK[k], :], w1[:, DI + 128 * k:DI + 128 * k + KT[k]], fxs[:, c, :],
                                  start=True, stop=True).then_inc(f_gate, 1)
                        if c:
                            pe.wait_ge(f_ag, L * (3 * NC_) + 3 * c - 2 + k + FREE)
                        pe.matmul(ps[0:KT[k], A_BANK[k], :], w1[:, 128 * k:128 * k + KT[k]], fxs[:, c, :],
                                  start=True, stop=True).then_inc(f_a, 1)
                    if c >= 2:
                        pe.wait_ge(f_x, f - 1 + FREE)
                    for k in range(3):
                        pe.wait_ge(f_ag, L * (3 * NC_) + 3 * c + k + 1 + FREE)
                        mm = pe.matmul(ps[:, 6 + c % 2, :], w2[0:KT[k], k, :], fg[0:KT[k], k, :], start=(k == 0), stop=(k == 2))
                    mm.then_inc(f_y, 1)
            pe.wait_ge(f_x, LAYERS * NC_ + FREE)
            for t in range(NT):
                mm = pe.transpose(tile(0, t), xT[:, 1 + t * P:1 + t * P + P], ident)
            assert did(mm) == C_T

        @block.vector
        def _(v):
            step = [0]

            def did(ins):
                step[0] += 1
                ins.then_inc(a_dve, 1)
                v.wait_ge(a_dve, step[0])
                return step[0]

            def link_(ins, count, base):
                count[0] += 1
                ins.then_inc(link, 1)
                v.wait_ge(link, base + count[0])

            def rsqrt(y, s, a, do):
                do(v.tensor_scalar(a.bitcast(I32), s.bitcast(I32), 1, None, ALU.arith_shift_right))
                do(v.tensor_scalar(y.bitcast(I32), a.bitcast(I32), -1.0, float(RSQRT_MAGIC), ALU.mult, ALU.add))
                for _ in range(NEWTON):
                    do(v.scalar_tensor_tensor(a, y, -0.5, y, ALU.mult, ALU.mult))
                    do(v.tensor_tensor(a, a, s, ALU.mult))
                    do(v.scalar_tensor_tensor(y, a, 1.5, y, ALU.add, ALU.mult))

            def centre(dst, src):
                do = did
                do(v.tensor_reduce(st[:, 0:NT], src, AX, ALU.add))
                do(v.tensor_scalar(st[:, 0:NT], st[:, 0:NT], -1.0 / D, None, ALU.mult))
                return do(v.tensor_tensor(dst, src, st[:, 0:NT].unsqueeze(2).broadcast_to([P, NT, D]), ALU.add))

            def normalise(dst, src, square, squared_step):
                v.wait_ge(a_act, squared_step)
                did(v.tensor_reduce(st[:, 0:NT], square, AX, ALU.add))
                did(v.tensor_scalar(st[:, 0:NT], st[:, 0:NT], 1.0 / D, LN_EPS, ALU.mult, ALU.add))
                rsqrt(st2[:, 0:NT], st[:, 0:NT], st3[:, 0:NT], did)
                return did(v.tensor_tensor(dst, src, st2[:, 0:NT].unsqueeze(2).broadcast_to([P, NT, D]), ALU.mult))

            def over_tiles(r):
                return r.unsqueeze(1).broadcast_to([P, NT, D])

            def quat_mul(dst, a, b, tmp, conj):
                sg = lambda i, c: SIGN[i][c] * (-1 if conj and PERM[i][c] else 1)
                for c in range(4):
                    did(v.scalar_tensor_tensor(dst[:, :, c], a[:, :, 0], float(sg(0, c)), b[:, :, c], ALU.mult, ALU.mult))
                for i in range(1, 4):
                    for c in range(4):
                        did(v.tensor_tensor(tmp, a[:, :, i], b[:, :, PERM[i][c]], ALU.mult))
                        n = did(v.tensor_tensor(dst[:, :, c], dst[:, :, c], tmp, ALU.add if sg(i, c) > 0 else ALU.subtract))
                return n

            quats = lambda b: b[:, 0:N].rearrange("p (q c) -> p q c", c=4)

            v.wait_ge(a_act, AA_EXPC)
            did(v.tensor_scalar(st[:, 2:3], st[:, 1:2], 1.0, None, ALU.add))
            did(v.reciprocal(st[:, 3:4], st[:, 2:3]))
            did(v.tensor_tensor(st[:, 4:5], st[:, 3:4], st[:, 0:1], ALU.mult))
            v.wait_ge(in_cst, 16)
            assert did(v.tensor_scalar(st2[:, 0:P], cst[:, C_ONE:C_ONE + P], st[:, 4:5], None, ALU.mult)) == AD_SILU
            v.wait_ge(a_pe, A_MOD)
            for j in range(2):
                did(v.tensor_copy(mod[:, 384 * j:384 * j + 384], ps[:, 6 + j, 0:384]))
            sa, ca, ga, sb_, cb, gb = (mod[:, D * j:D * j + D] for j in range(6))
            for m in (ca, cb):
                did(v.tensor_scalar(m, m, 1.0, None, ALU.add))
            for m in (ga, gb):
                did(v.tensor_scalar(st3[:, 0:D], m, 0.0, None, ALU.is_ge))
                did(v.tensor_scalar(st3[:, 0:D], st3[:, 0:D], 2.0, -1.0, ALU.mult, ALU.add))
                did(v.tensor_scalar(st3[:, D:2 * D], m, -1.0, 0.25, ALU.mult, ALU.max))
                did(v.tensor_tensor(m, m, st3[:, D:2 * D], ALU.max))
                n = did(v.tensor_tensor(m, m, st3[:, 0:D], ALU.mult))
            assert n == AD_MOD, n
            v.wait_ge(in_x, 16)
            n = centre(tok(t1), x1[:, :, :])
            assert n == AD_XC1, n
            normalise(tok(t1), tok(t1), tok(t2), AA_SQ1)
            did(v.tensor_tensor(tok(t1), tok(t1), over_tiles(ca), ALU.mult))
            n = did(v.tensor_tensor(tok(sq), tok(t1), over_tiles(sa), ALU.add))
            assert n == AD_H, n
            v.wait_ge(a_pe, A_KV)
            did(v.tensor_copy(h_keep, sq[:, 0:N]))
            kv = ps[:, :, :].rearrange("p b (t n) -> p (b t) n", n=256)
            did(v.tensor_tensor(tok(t2), kv[:, :, D:2 * D], over_tiles(row[:, R_BKV + D:R_BKV + 2 * D]), ALU.add))
            n = did(v.tensor_tensor(tok(t1), kv[:, :, 0:D], over_tiles(row[:, R_BKV:R_BKV + D]), ALU.add))
            assert n == AD_KV, n
            v.wait_ge(a_act, AA_KSQ)
            did(v.tensor_reduce(st[:, :], quats(sq), AX, ALU.add))
            did(v.tensor_scalar(st[:, :], st[:, :], NORM_GUARD, None, ALU.max))
            rsqrt(st2[:, :], st[:, :], st3[:, :], did)
            did(v.tensor_tensor(quats(t1), quats(t1), st2[:, :].unsqueeze(2).broadcast_to([P, NQ, 4]), ALU.mult))
            quat_mul(quats(u), quats(t2), quats(t1), st[:, :], False)
            n = did(v.tensor_copy(pre[:, 1, :], tok(u)[:, 0, :]))
            for t in range(2, NT):
                n = did(v.tensor_tensor(pre[:, t, :], pre[:, t - 1, :], tok(u)[:, t - 1, :], ALU.add))
            assert n == AD_PRE, n
            v.wait_ge(a_act, AA_MEM)
            quat_mul(quats(sq), quats(t2), quats(t1), st[:, :], True)
            did(v.tensor_tensor(tok(sq), tok(sq), cst[:, C_RSQ:C_RSQ + NT].unsqueeze(2).broadcast_to([P, NT, D]), ALU.mult))
            n = centre(tok(u), tok(sq))
            assert n == AD_XC2, n
            normalise(tok(u), tok(u), tok(t2), AA_SQ2)
            did(v.tensor_tensor(tok(u), tok(u), over_tiles(row[:, R_G:R_G + D]), ALU.mult))
            n = did(v.tensor_tensor(tok(u), tok(u), over_tiles(row[:, R_B:R_B + D]), ALU.add))
            assert n == AD_N, n
            v.wait_ge(a_pe, A_WO)
            y = ps[:, 0:4, :].rearrange("p b (t d) -> p (b t) d", d=D)
            did(v.tensor_tensor(tok(t1), y, over_tiles(row[:, R_BO:R_BO + D]), ALU.add))
            did(v.tensor_tensor(t1[:, 0:N], t1[:, 0:N], h_keep, ALU.add))
            did(v.tensor_tensor(tok(t1), tok(t1), over_tiles(ga), ALU.mult))
            did(v.tensor_tensor(x1[:, :, :], x1[:, :, :], tok(t1), ALU.add))
            n = centre(tok(t1), x1[:, :, :])
            assert n == AD_XC3, n
            normalise(tok(t1), tok(t1), tok(t2), AA_SQ3)
            did(v.tensor_tensor(tok(t1), tok(t1), over_tiles(cb), ALU.mult))
            n = did(v.tensor_tensor(tok(t1), tok(t1), over_tiles(sb_), ALU.add))
            assert n == AD_H2, n

            def stage(t, g):
                v.wait_ge(proj_done, g * 6 + FREE)
                v.tensor_scalar(xs[0:64, :], xT[0:64, bass.ds(t * P + 1, P)], 1.0, None, ALU.mult).then_inc(xs_ready, 1)
                v.tensor_scalar(xs[64:P, :], xT[64:P, bass.ds(t * P, P)], 1.0, None, ALU.mult).then_inc(xs_ready, 1)

            tq = lambda t, j, lo, hi: tabl[:, bass.ds(t, 1), j * DH + lo:j * DH + hi].broadcast_to([P, 8, hi - lo])

            def rotate(t, g):
                v.wait_ge(added, g * 4 + FREE)
                for c in range(4):
                    v.wait_ge(squared, g * 4 + c + 1)
                    q = ps[:, c % 2, :].rearrange("p (h d) -> p h d", d=DH)
                    a, b = (x[:, c * 512:c * 512 + 512].rearrange("p (h d) -> p h d", d=DH) for x in (t1, t2))
                    j = 2 * (c // 2)
                    v.tensor_tensor(a, q, tq(t, j, 0, DH), ALU.mult)
                    v.tensor_tensor(b[:, :, 0:32], q[:, :, 32:64], tq(t, j + 1, 0, 32), ALU.mult)
                    v.tensor_tensor(b[:, :, 32:64], q[:, :, 0:32], tq(t, j + 1, 32, 64), ALU.mult).then_inc(rotated, 1)

            def norms(g):
                n = [0]
                do = lambda ins: link_(ins, n, g * NORM_LINKS)
                v.wait_ge(squared, g * 4 + 4)
                v.tensor_reduce(ss[:, :], sq[:, :].rearrange("p (h d) -> p h d", d=DH), AX, ALU.add).then_inc(inv_norm, 1)
                v.wait_ge(inv_norm, g + 1 + FREE)
                do(v.tensor_scalar(ss[:, :], ss[:, :], NORM_GUARD, None, ALU.max))
                rsqrt(rn[:, :], ss[:, :], ra[:, :], do)
                assert n[0] == NORM_LINKS, n
                for j, done in enumerate((q_normed, k_normed)):
                    v.wait_ge(added, g * 4 + 2 + 2 * j + FREE)
                    x = u[:, j * INNER:(j + 1) * INNER].rearrange("p (h d) -> p h d", d=DH)
                    v.tensor_tensor(x, x, rn[:, j * H:(j + 1) * H].unsqueeze(2).broadcast_to([P, H, DH]), ALU.mult).then_inc(done, 1)

            def shift_by_max(g):
                v.wait_ge(scored, g + 1 + FREE)
                v.wait_ge(p_trans, g * 2 + FREE)
                s = ps[:, 4:6, :].rearrange("p b (h n) -> p (b h) n", n=2 * W)
                v.tensor_reduce(mx[:, :], s, AX, ALU.max).then_inc(max_ready, 1)
                v.wait_ge(max_ready, g + 1)
                v.tensor_tensor(pr[:, :, :], s, mx[:, :].unsqueeze(2).broadcast_to([P, H, 2 * W]), ALU.subtract).then_inc(shifted, 1)

            def inv_sums(g):
                v.wait_ge(exp_done, g + 1)
                v.tensor_reduce(rs[:, :], pr[:, :, :], AX, ALU.add).then_inc(sum_ready, 1)
                v.wait_ge(sum_ready, g + 1)
                v.reciprocal(ri[:, :], rs[:, :]).then_inc(rsum_ready, 1)

            def output(g):
                v.wait_ge(rsum_ready, g + 1)
                v.wait_ge(av_done, g + 1 + FREE)
                v.wait_ge(o_trans, g * 2 + FREE)
                a = ps[:, 6:8, :].rearrange("p b (h n) -> p (b h) n", n=DH)
                v.tensor_tensor(o.rearrange("p (h n) -> p h n", n=DH), a,
                                ri[:, :].unsqueeze(2).broadcast_to([P, H, DH]), ALU.mult).then_inc(o_normed, 1)

            def add_x(t, g):
                v.wait_ge(y_done, g + 1 + FREE)
                xt = xT[:, bass.ds(t * P + 1, P)]
                v.tensor_tensor(xt, ps[:, 2, 0:P], xt, ALU.add).then_inc(x_added, 1)

            v.wait_ge(in_prm, 16)
            v.wait_ge(a_act, A_XT)
            with v.Fori(0, LAYERS) as L:
                v.wait_ge(f_x, L * NC_ + FREE)
                v.tensor_copy(pl[:, :], prm[:, bass.ds(L, 1), :].rearrange("p a n -> p (a n)")).then_inc(f_prm, 1)
                stage(0, L * NT)
                v.wait_ge(tabs_ready, L + 1)
                rotate(0, L * NT)
                norms(L * NT)
                with v.Fori(0, NT - 1) as t:
                    g = L * NT + t
                    stage(t + 1, g + 1)
                    shift_by_max(g)
                    rotate(t + 1, g + 1)
                    inv_sums(g)
                    norms(g + 1)
                    output(g)
                    add_x(t, g)
                g = L * NT + (NT - 1)
                shift_by_max(g)
                inv_sums(g)
                output(g)
                add_x(NT - 1, g)
                v.wait_ge(x_added, L * NT + NT + FREE)
                for c in range(NC_):
                    v.tensor_copy(fxs[0:64, c, :], xT[0:64, 1 + c * CH:1 + c * CH + CH]).then_inc(f_xs, 1)
                    v.tensor_copy(fxs[64:P, c, :], xT[64:P, c * CH:c * CH + CH]).then_inc(f_xs, 1)
                for c in range(NC_):
                    f = L * NC_ + c
                    v.wait_ge(f_sq, f + 1)
                    v.tensor_copy(fxc[:, c, :], ps[:, c % 2, :]).then_inc(f_cp, 1)
                for c in range(NC_):
                    f = L * NC_ + c
                    v.wait_ge(f_std, f + 1)
                    v.reciprocal(fsq[:, c, :], fsq[:, c, :]).then_inc(f_rstd, 1)
                    v.wait_ge(f_rstd, f + 1)
                    v.tensor_tensor(fxs[:, c, :], fxc[:, c, :], fsq[:, c, :], ALU.mult).then_inc(f_xn, 1)
                    v.wait_ge(f_xn, f + 1)
                    v.wait_ge(f_prm, L + 1)
                    v.tensor_scalar(fxs[:, c, :], fxs[:, c, :], pl[:, L_G:L_G + 1], pl[:, L_B:L_B + 1], ALU.mult, ALU.add).then_inc(f_aff, 1)
                for c in range(NC_):
                    f = L * NC_ + c
                    for k in range(3):
                        i = L * (3 * NC_) + 3 * c + k + 1
                        v.wait_ge(f_a, i)
                        v.wait_ge(f_gelu, i)
                        g_ = fg[0:KT[k], k, :]
                        v.scalar_tensor_tensor(g_, ps[0:KT[k], A_BANK[k], :], pl[0:KT[k], L_BA + k:L_BA + k + 1], g_,
                                               ALU.add, ALU.mult).then_inc(f_ag, 1)
                    v.wait_ge(f_y, f + 1 + FREE)
                    xt = xT[:, 1 + c * CH:1 + c * CH + CH]
                    v.scalar_tensor_tensor(xt, ps[:, 6 + c % 2, :], pl[:, L_B2:L_B2 + 1], xt, ALU.add, ALU.add).then_inc(f_x, 1)
            v.wait_ge(a_pe, C_T)
            y = ps[:, 0:4, :].rearrange("p b (t d) -> p (b t) d", d=D)
            did(v.tensor_tensor(tok(t1), y, over_tiles(gb), ALU.mult))
            n = did(v.tensor_tensor(x1[:, :, :], x1[:, :, :], tok(t1), ALU.add))
            assert n == C_OUT, n




def rotary_tables():
    f = np.float32
    half = np.arange(0, DH, 2, dtype=f)
    inv_freq = (f(1) / np.power(f(10000), half / f(DH))).astype(f)
    pos = np.arange(N, dtype=f)
    freqs = (pos[:, None] * inv_freq[None, :]).astype(f).astype(np.float64)
    base = ((half + f(0.4 * DH)) / f(1.4 * DH)).astype(np.float64)
    scale = base[None, :] ** ((np.arange(N) % P - P // 2) / (W // 2))[:, None]
    cos, sin = np.cos(freqs), np.sin(freqs)
    parts = []
    for s in (scale, 1.0 / scale):
        parts += [cos * s, cos * s, -sin * s, sin * s]
    carry = np.tile(base ** (P / (W // 2)), P // len(base))
    return np.concatenate(parts, 1).astype(f), carry.astype(f)


def constants(carry):
    c = np.zeros((P, C_END), np.float32)
    i = np.arange(P)
    c[:, C_ID:C_ID + P] = np.eye(P)
    c[:, C_TRI:C_TRI + P] = i[:, None] <= i[None, :]
    c[:, C_ONE:C_ONE + P] = 1
    c[:, C_AVG:C_AVG + P] = 1 / D
    c[:, C_CEN:C_CEN + P] = np.eye(P) - 1 / D
    q, k = i[:, None] % W, np.arange(2 * W)[None, :]
    seen = (k >= q) & (k <= q + W)
    c[:, C_MASK:C_MASK + 2 * W] = np.where(seen, 0, MASKED)
    c[:, C_MASK0:C_MASK0 + 2 * W] = np.where(seen & ((i[:, None] >= W) | (k >= W)), 0, MASKED)
    c[:, C_KS] = carry
    c[:, C_RSQ:C_RSQ + NT] = 1 / np.sqrt(np.arange(1, N + 1).reshape(NT, P).T)
    c[:, C_EPS] = LN_EPS
    return c


def kernel(**inputs):
    import concourse.bacc as bacc
    from concourse.bass_utils import run_bass_kernel_spmd

    a = {k: np.asarray(v) for k, v in inputs.items()}
    f = np.float32
    tab, carry = rotary_tables()
    wqkv = a["L0_ffn_Wqkv"]
    v = wqkv[:, :, 2 * INNER:].reshape(LAYERS, D, HP, 2, DH).transpose(0, 1, 3, 2, 4).reshape(LAYERS, D, INNER)
    qs, ks = a["L0_ffn_q_scale"], a["L0_ffn_k_scale"]
    swap = lambda s: np.concatenate([s[:, DH // 2:], s[:, :DH // 2]], 1)
    w2 = np.zeros((LAYERS, 3 * P, D), f)
    w2[:, :DI] = a["L0_ffn_W2"]
    prm = np.zeros((P, LAYERS, L_END), f)
    prm[:, :, L_G], prm[:, :, L_B], prm[:, :, L_B2] = a["L0_ffn_ln_g"].T, a["L0_ffn_ln_b"].T, a["L0_ffn_b2"].T
    for k, n in enumerate(KT):
        prm[:n, :, L_BA + k] = a["L0_ffn_b1"][:, P * k:P * k + n].T
        prm[:n, :, L_BG + k] = a["L0_ffn_b1"][:, DI + P * k:DI + P * k + n].T
    arrays = {
        "x": a["L0_attn_x"][0],
        "cst": constants(carry),
        "row": np.concatenate([a["L0_attn_bk"], a["L0_attn_bv"], a["L0_attn_ln_g"], a["L0_attn_ln_b"], a["L0_attn_bo"]]),
        "c": a["L0_c"].reshape(D, 1),
        "wmod": a["L0_wmod"],
        "wkv": np.concatenate([a["L0_attn_Wk"].T, a["L0_attn_Wv"].T], 1),
        "woa": a["L0_attn_Wo"].T,
        "tab": tab,
        "scl": np.concatenate([qs, swap(qs), ks, swap(ks)], 1),
        "wqkv": np.concatenate([wqkv[:, :, :2 * INNER], v], 2).reshape(LAYERS * D, 3 * INNER),
        "wo": a["L0_ffn_Wo"].reshape(LAYERS, HP, P, D).transpose(0, 2, 1, 3).reshape(LAYERS * P, HP * D),
        "w1": a["L0_ffn_W1"].reshape(LAYERS * D, 2 * DI),
        "w2": w2.reshape(LAYERS, 3, P, D).transpose(0, 2, 1, 3).reshape(LAYERS * P, 3 * D),
        "prm": prm,
    }
    arrays = {f"in_{k}": np.ascontiguousarray(x) for k, x in arrays.items()}
    nc = bacc.Bacc("TRN2", target_bir_lowering=False, num_devices=1)
    args = [nc.dram_tensor(k, x.shape, mybir.dt.from_np(x.dtype), kind="ExternalInput").ap() for k, x in arrays.items()]
    out = nc.dram_tensor("out", [N, D], F32, kind="ExternalOutput").ap()
    program(nc, *args, out)
    r = run_bass_kernel_spmd(nc, [arrays], core_ids=[0])
    return r.results[0]["out"].reshape(1, N, D)
```

```python
import numpy as np
import concourse.bass as bass
from concourse import mybir
from contextlib import ExitStack

F32 = mybir.dt.float32
BF16 = mybir.dt.bfloat16
I32 = mybir.dt.int32
ALU = mybir.AluOpType
ACT = mybir.ActivationFunctionType
AX = mybir.AxisListType.X

N, D = 2048, 128
P = 128
NT = N // P
LAYERS, H, DH, W = 6, 16, 64, 32
HP = H // 2
NW = P // W
INNER = H * DH
DI = 341
CH = 512
NC_ = N // CH
NQ = N * D // (P * 4)
KT = [128, 128, DI - 256]
LN_EPS = 1e-5
NORM_GUARD = 1e-24
MASKED = -1e30
RSQRT_MAGIC = 0x5F3759DF

C_ID, C_TRI, C_ONE, C_AVG, C_CEN, C_MASK, C_MASK0 = 0, 128, 256, 384, 512, 640, 704
C_KS, C_RSQ, C_EPS, C_END = 768, 769, 785, 786
R_BKV, R_G, R_B, R_BO, R_END = 0, 256, 384, 512, 640
L_G, L_B, L_B2, L_BA, L_BG, L_END = 0, 1, 2, 3, 6, 9

GATE_BANK, A_BANK = [0, 1, 2], [3, 4, 5]
QK_BANK, V_BANK = [0, 1, 6, 7], [2, 3]
AD_SILU, AD_MOD, AD_XC1, AD_H, AD_KV, AD_PRE, AD_XC2, AD_N, AD_XC3, AD_H2, C_OUT = 4, 18, 21, 37, 40, 97, 129, 145, 152, 168, 170
AA_EXPC, AA_SQ1, AA_HT, AA_KSQ, AA_MEM, AA_SQ2, AA_NT, AA_SQ3, A_XT = range(1, 10)
A_MOD, A_T1, A_KV, A_CUM, A_T2, A_WO, A_T3, C_T = range(1, 9)
FREE = 1
NEWTON = 3
NORM_LINKS = 1 + 2 + 3 * NEWTON

PERM = [[0, 1, 2, 3], [1, 0, 3, 2], [2, 3, 0, 1], [3, 2, 1, 0]]
SIGN = [[1, 1, 1, 1], [-1, 1, -1, 1], [-1, 1, 1, -1], [-1, -1, 1, 1]]


def program(nc, x_d, cst_d, row_d, c_d, wmod_d, wkv_d, woa_d, tab_d, scl_d, wqkv_d, wo_d, w1_d, w2_d, prm_d,
            out_d):
    ctx = ExitStack()
    with ctx:
        def sb(name, shape, dt=F32):
            return ctx.enter_context(nc.sbuf_tensor(name, shape, dt))

        def sem(name):
            return ctx.enter_context(nc.semaphore(name))

        cst = sb("cst", [P, C_END])
        row = sb("row", [P, R_END])
        maskb = sb("maskb", [P, 2, 8, 2 * W], BF16)
        identb = sb("identb", [P, P], BF16)
        mod = sb("mod", [P, 6 * D])
        x1 = sb("x1", [P, NT, D])
        xT = sb("xT", [P, 1 + N])
        wbuf = sb("wbuf", [P, 3 * INNER])
        wo = sb("wo", [P, HP, D])
        w1 = sb("w1", [P, 2 * DI])
        w2 = sb("w2", [P, 3, D])
        prm = sb("prm", [P, LAYERS, L_END])
        pl = sb("pl", [P, L_END])
        scl = sb("scl", [P, LAYERS, 4 * DH])
        tab = sb("tab", [P, NT, 4 * DH])
        tabl = sb("tabl", [P, NT, 4 * DH])
        xs = sb("xs", [P, P])
        sq = sb("sq", [P, 2 * INNER])
        tr = sb("tr", [P, 4, 2, 512])
        t1, t2 = (tr[:, 2 * j:2 * j + 2, :, :].rearrange("p a b n -> p (a b n)") for j in range(2))
        u = sb("u", [P, 2 * INNER])
        ss = sb("ss", [P, 2 * H])
        rn = sb("rn", [P, 2 * H])
        ra = sb("ra", [P, 2 * H])
        vs = sb("vs", [P, 2, HP * DH])
        vf = sb("vf", [P, 2, NW, HP * DH])
        qT = sb("qT", [P, HP, P])
        kT = sb("kT", [P, 2, HP, W + P])
        pr = sb("pr", [P, H, 2 * W])
        mx = sb("mx", [P, H])
        rs = sb("rs", [P, H])
        ri = sb("ri", [P, H])
        pT = sb("pT", [P, HP, P])
        od = sb("od", [P, 2 * INNER])
        o = od[:, 0:INNER]
        oT = od[:, INNER:2 * INNER].rearrange("p (k n) -> p k n", n=P)
        st = sb("st", [P, 512])
        st2 = sb("st2", [P, 512])
        st3 = sb("st3", [P, 512])
        tok = lambda b: b[:, 0:N].rearrange("p (t d) -> p t d", d=D)
        h_keep = od[:, :]
        pre = xT[:, 1:1 + N].rearrange("p (t d) -> p t d", d=D)
        ps = ctx.enter_context(nc.psum_tensor("ps", [P, 8, 512], F32))

        v_scr = nc.dram_tensor("v_scratch", [W + N, 2 * HP * DH], F32, kind="Internal").ap()

        in_x, in_cst, in_vec, in_wa = sem("in_x"), sem("in_cst"), sem("in_vec"), sem("in_wa")
        in_tab, in_prm, zero_row = sem("in_tab"), sem("in_prm"), sem("zero_row")
        in_wqkv, in_wo, in_w12 = sem("in_wqkv"), sem("in_wo"), sem("in_w12")
        cleared, tabs_ready, masks_ready = sem("cleared"), sem("tabs_ready"), sem("masks_ready")
        a_dve, a_act, a_pe = sem("a_dve"), sem("a_act"), sem("a_pe")
        xs_ready, proj_done, v_evac = sem("xs_ready"), sem("proj_done"), sem("v_evac")
        v_stored, v_frames = sem("v_stored"), sem("v_frames")
        squared, rotated, added, sq_summed, link = sem("squared"), sem("rotated"), sem("added"), sem("sq_summed"), sem("link")
        q_normed, k_normed, q_trans, k_trans = sem("q_normed"), sem("k_normed"), sem("q_trans"), sem("k_trans")
        q_evac, k_evac, k_carried = sem("q_evac"), sem("k_evac"), sem("k_carried")
        scored, max_ready, shifted, exp_done = sem("scored"), sem("max_ready"), sem("shifted"), sem("exp_done")
        sum_ready, rsum_ready = sem("sum_ready"), sem("rsum_ready")
        p_trans, p_evac, av_done, o_normed = sem("p_trans"), sem("p_evac"), sem("av_done"), sem("o_normed")
        o_trans, o_evac, y_done, x_added = sem("o_trans"), sem("o_evac"), sem("y_done"), sem("x_added")
        f_xs, f_cen, f_sq, f_var, f_cp = sem("f_xs"), sem("f_cen"), sem("f_sq"), sem("f_var"), sem("f_cp")
        f_std, f_rstd, f_xn, f_aff, f_prm = sem("f_std"), sem("f_rstd"), sem("f_xn"), sem("f_aff"), sem("f_prm")
        f_gate, f_a, f_gelu, f_ag, f_y, f_x = sem("f_gate"), sem("f_a"), sem("f_gelu"), sem("f_ag"), sem("f_y"), sem("f_x")
        out_done = sem("out_done")

        ident = cst[:, C_ID:C_ID + P]
        block = ctx.enter_context(nc.Block())

        fxs = sq[:, 0:N].rearrange("p (c n) -> p c n", n=CH)
        fsq = t1[:, 0:N].rearrange("p (c n) -> p c n", n=CH)
        fxc = t2[:, 0:N].rearrange("p (c n) -> p c n", n=CH)
        fg = u[:, 0:3 * CH].rearrange("p (k n) -> p k n", n=CH)
        avg = cst[:, C_AVG:C_AVG + P]
        cen = cst[:, C_CEN:C_CEN + P]

        @block.sync
        def _(sp):
            for s in (v_evac, k_normed, v_frames, av_done, y_done, proj_done, k_trans, scored, rotated, v_stored, sq_summed,
                      f_ag, f_y, shifted, x_added, o_normed, added, p_trans, o_trans, f_x):
                sp.sem_inc(s, FREE)
            sp.dma_start(x1[:, :, :], x_d.rearrange("(t p) d -> p t d", p=P)).then_inc(in_x, 16)
            sp.dma_start(cst[:, :], cst_d).then_inc(in_cst, 16)
            sp.dma_start(st[:, 0:1], c_d).then_inc(in_vec, 16)
            sp.dma_start(wo[:, 0:6, :], wmod_d.rearrange("p (a d) -> p a d", d=D)).then_inc(in_vec, 16)
            sp.dma_start(row[:, :], row_d.partition_broadcast(P)).then_inc(in_vec, 16)
            sp.dma_start(w1[:, 0:256], wkv_d).then_inc(in_wa, 16)
            sp.dma_start(w1[:, 256:384], woa_d).then_inc(in_wa, 16)
            sp.dma_start(scl[:, :, :], scl_d.partition_broadcast(P)).then_inc(in_tab, 16)
            sp.dma_start(tab[:, :, :], tab_d.rearrange("(t p) c -> p t c", p=P)).then_inc(in_tab, 16)
            sp.dma_start(prm[:, :, :], prm_d).then_inc(in_prm, 16)
            sp.wait_ge(cleared, 1)
            sp.dma_start(v_scr[0:W, :], vf[0:W, 0, 0:2, :].rearrange("p w n -> p (w n)")).then_inc(zero_row, 16)
            sp.wait_ge(zero_row, 16)
            sp.wait_ge(a_pe, A_MOD)
            with sp.Fori(0, LAYERS) as L:
                rows, n_proj, n_y, n_xs = (sp.snap(x) for x in (L * P, L * (6 * NT) + FREE, L * NT + FREE, L * (2 * NT) + 2))
                sp.wait_ge(proj_done, n_proj)
                sp.dma_start(wbuf[:, :], wqkv_d[bass.ds(rows, P), :]).then_inc(in_wqkv, 16)
                sp.wait_ge(y_done, n_y)
                sp.dma_start(wo[:, :, :], wo_d[bass.ds(rows, P), :].rearrange("p (k d) -> p k d", d=D)).then_inc(in_wo, 16)
                sp.wait_ge(xs_ready, n_xs)
                sp.dma_start(w1[:, :], w1_d[bass.ds(rows, P), :]).then_inc(in_w12, 16)
                sp.dma_start(w2[:, :, :], w2_d[bass.ds(rows, P), :].rearrange("p (k d) -> p k d", d=D)).then_inc(in_w12, 16)
                with sp.Fori(0, NT) as t:
                    g = L * NT + t
                    even, odd, n_v, n_fr, n_st, n_av = (sp.snap(x) for x in (t * P, t * P + W, g * 2 + 2 + FREE, g * 64 + FREE, g * 16 + 16 + FREE, g + FREE))
                    sp.wait_ge(v_frames, n_fr)
                    sp.wait_ge(v_evac, n_v)
                    sp.dma_start(v_scr[bass.ds(odd, P), :], vs[:, :, :].rearrange("p a n -> p (a n)")).then_inc(v_stored, 16)
                    sp.wait_ge(av_done, n_av)
                    sp.wait_ge(v_stored, n_st)
                    for a in range(2):
                        for w, first in enumerate((even, odd)):
                            src = v_scr[bass.ds(first, P), a * HP * DH:(a + 1) * HP * DH]
                            sp.dma_start(vf[DH * a:DH * a + DH, a, w:NW:2, :],
                                         src.rearrange("(w p) n -> p w n", p=2 * W)).then_inc(v_frames, 16)
            sp.wait_ge(a_dve, C_OUT)
            sp.dma_start(out_d.rearrange("(t p) d -> p t d", p=P), x1[:, :, :]).then_inc(out_done, 16)
            sp.wait_ge(out_done, 16)
            sp.wait_ge(v_stored, LAYERS * NT * 16 + FREE)
            sp.wait_ge(v_frames, LAYERS * NT * 64 + FREE)

        @block.gpsimd
        def _(pool):
            pool.memset(vf[:, :, :, :], 0.0).then_inc(cleared, 1)
            pool.memset(kT[:, :, :, :], 0.0).then_inc(cleared, 1)
            pool.memset(xT[:, 0:1], 0.0).then_inc(cleared, 1)
            pool.wait_ge(in_cst, 16)
            pool.tensor_copy(identb[:, :], ident).then_inc(masks_ready, 1)
            for m, c in enumerate((C_MASK, C_MASK0)):
                pool.tensor_copy(maskb[:, m, :, :], cst[:, c:c + 2 * W].unsqueeze(1).broadcast_to([P, 8, 2 * W])).then_inc(masks_ready, 1)
            def finish_qk(g):
                pool.wait_ge(k_trans, g * 2 + FREE)
                uh = u[:, :].rearrange("p (j c h d) -> p j c h d", j=2, c=2, d=DH)
                th = tr[:, :, :, :].rearrange("p (j c) s (h d) -> p j c s h d", j=2, d=DH)
                for j in range(2):
                    pool.wait_ge(rotated, g * 4 + 2 * j + 2 + FREE)
                    for x in range(2):
                        lo, hi = slice(32 * x, 32 * x + 32), slice(32 - 32 * x, 64 - 32 * x)
                        pool.tensor_tensor(uh[:, j, :, :, lo], th[:, j, :, 0, :, lo], th[:, j, :, 1, :, hi], ALU.add).then_inc(added, 1)
                pool.wait_ge(link, g * NORM_LINKS + NORM_LINKS)
                for j, done in enumerate((q_normed, k_normed)):
                    pool.wait_ge(added, g * 4 + 2 * j + 2 + FREE)
                    x = u[:, j * INNER:(j + 1) * INNER].rearrange("p (h d) -> p h d", d=DH)
                    pool.tensor_tensor(x, x, rn[:, j * H:(j + 1) * H].unsqueeze(2).broadcast_to([P, H, DH]), ALU.mult).then_inc(done, 1)

            pool.wait_ge(in_tab, 32)
            with pool.Fori(0, LAYERS) as L:
                pool.wait_ge(rotated, L * (4 * NT) + FREE)
                pool.tensor_tensor(tabl[:, :, :], tab[:, :, :],
                                   scl[:, bass.ds(L, 1), :].broadcast_to([P, NT, 4 * DH]), ALU.mult).then_inc(tabs_ready, 1)
                finish_qk(L * NT)
                finish_qk(L * NT + 1)
                with pool.Fori(0, NT - 2) as t:
                    finish_qk(L * NT + t + 2)

        @block.scalar
        def _(act):
            step = [0]

            def did(ins, sem_=a_act):
                step[0] += 1
                ins.then_inc(sem_, 1)
                return step[0]

            act.wait_ge(in_vec, 48)
            assert did(act.activation(st[:, 1:2], st[:, 0:1], ACT.Exp, scale=-1.0)) == AA_EXPC
            act.wait_ge(a_dve, AD_XC1)
            assert did(act.activation(tok(t2), tok(t1), ACT.Square)) == AA_SQ1
            act.wait_ge(a_pe, A_T1)
            assert did(act.activation(u[:, 0:N], ps[:, 0:4, :].rearrange("p b n -> p (b n)"), ACT.Copy)) == AA_HT
            act.wait_ge(a_dve, AD_KV)
            assert did(act.activation(sq[:, 0:N], t1[:, 0:N], ACT.Square)) == AA_KSQ
            act.wait_ge(a_pe, A_CUM)
            assert did(act.activation(t2[:, 0:N], ps[:, 0:4, :].rearrange("p b n -> p (b n)"), ACT.Copy)) == AA_MEM
            act.wait_ge(a_dve, AD_XC2)
            assert did(act.activation(tok(t2), tok(u), ACT.Square)) == AA_SQ2
            act.wait_ge(a_pe, A_T2)
            assert did(act.activation(t1[:, 0:N], ps[:, 4:8, :].rearrange("p b n -> p (b n)"), ACT.Copy)) == AA_NT
            act.wait_ge(a_dve, AD_XC3)
            assert did(act.activation(tok(t2), tok(t1), ACT.Square)) == AA_SQ3
            act.wait_ge(a_pe, A_T3)
            act.wait_ge(cleared, 3)
            assert did(act.activation(xT[:, 1:1 + N], ps[:, 4:8, :].rearrange("p b n -> p (b n)"), ACT.Copy)) == A_XT

            def evac_v(g):
                act.wait_ge(v_stored, g * 16 + FREE)
                for a in range(2):
                    act.wait_ge(proj_done, g * 6 + a + 5 + FREE)
                    act.activation(vs[:, a, :], ps[:, V_BANK[a], :], ACT.Copy).then_inc(v_evac, 1)

            def squares(g, chunks):
                act.wait_ge(sq_summed, g + FREE)
                for c in chunks:
                    act.wait_ge(proj_done, g * 6 + c + 1 + FREE)
                    act.activation(sq[:, c * 512:c * 512 + 512], ps[:, QK_BANK[c], :], ACT.Square).then_inc(squared, 1)

            def probabilities(g):
                act.wait_ge(shifted, g + 1 + FREE)
                act.activation(pr[:, :, :], pr[:, :, :], ACT.Exp, scale=8.0).then_inc(exp_done, 1)

            def evac_p(g):
                act.wait_ge(av_done, g + FREE)
                for b in range(2):
                    act.wait_ge(p_trans, g * 2 + b + 1 + FREE)
                    act.activation(pT[:, 4 * b:4 * b + 4, :], bank(2 + b), ACT.Copy).then_inc(p_evac, 1)

            def evac_q(g):
                act.wait_ge(scored, g + FREE)
                act.activation(kT[:, :, :, 0:W], kT[:, :, :, P:P + W], ACT.Copy, scale=cst[:, C_KS:C_KS + 1]).then_inc(k_carried, 1)
                for b in range(2):
                    act.wait_ge(q_trans, g * 2 + b + 1)
                    act.activation(qT[:, 4 * b:4 * b + 4, :], bank(2 + b), ACT.Copy).then_inc(q_evac, 1)

            def evac_k(g, b):
                act.wait_ge(k_carried, g + 1)
                act.wait_ge(k_trans, g * 2 + b + 1 + FREE)
                for a in range(2):
                    r = slice(DH * a, DH * a + DH)
                    act.activation(kT[r, a, 4 * b:4 * b + 4, W:W + P], bank(b)[r], ACT.Copy).then_inc(k_evac, 1)

            def evac_o(g):
                act.wait_ge(y_done, g + FREE)
                for b in range(2):
                    act.wait_ge(o_trans, g * 2 + b + 1 + FREE)
                    act.activation(oT[:, 4 * b:4 * b + 4, :], bank(2 + b), ACT.Copy).then_inc(o_evac, 1)

            def bank(b):
                return ps[:, b, :].rearrange("p (a n) -> p a n", n=P)

            with act.Fori(0, LAYERS) as L:
                for t in range(2):
                    squares(L * NT + t, range(4))
                    evac_v(L * NT + t)
                evac_q(L * NT)
                evac_k(L * NT, 0)
                evac_k(L * NT, 1)
                with act.Fori(0, NT - 2) as t:
                    g = L * NT + t
                    squares(g + 2, (0, 1))
                    probabilities(g)
                    squares(g + 2, (2, 3))
                    evac_v(g + 2)
                    evac_p(g)
                    evac_q(g + 1)
                    evac_k(g + 1, 0)
                    evac_o(g)
                    evac_k(g + 1, 1)
                for t in (NT - 2, NT - 1):
                    g = L * NT + t
                    probabilities(g)
                    evac_p(g)
                    if t < NT - 1:
                        evac_q(g + 1)
                        evac_k(g + 1, 0)
                    evac_o(g)
                    if t < NT - 1:
                        evac_k(g + 1, 1)
                def square(c):
                    act.wait_ge(f_cen, L * NC_ + c + 1)
                    act.activation(fsq[:, c, :], ps[:, c % 2, :], ACT.Square).then_inc(f_sq, 1)

                def deviation(c):
                    act.wait_ge(f_var, L * NC_ + c + 1)
                    act.activation(fsq[:, c, :], ps[:, 2 + c % 2, :], ACT.Sqrt, bias=cst[:, C_EPS:C_EPS + 1]).then_inc(f_std, 1)

                square(0)
                for c in range(NC_):
                    if c + 1 < NC_:
                        square(c + 1)
                    deviation(c)
                for c in range(NC_):
                    act.wait_ge(f_ag, L * (3 * NC_) + 3 * c + FREE)
                    act.wait_ge(f_y, L * NC_ + c + FREE)
                    for k in range(3):
                        act.wait_ge(f_gate, L * (3 * NC_) + 3 * c + k + 1)
                        act.activation(fg[0:KT[k], k, :], ps[0:KT[k], GATE_BANK[k], :], ACT.Gelu,
                                       bias=pl[0:KT[k], L_BG + k:L_BG + k + 1]).then_inc(f_gelu, 1)

        @block.tensor
        def _(pe):
            step = [0]

            def did(ins):
                step[0] += 1
                ins.then_inc(a_pe, 1)
                return step[0]

            def tile(b, t):
                return ps[:, b + t // 4, (t % 4) * P:(t % 4) * P + P]

            pe.wait_ge(a_dve, AD_SILU)
            for j in range(2):
                mm = pe.matmul(ps[:, 6 + j, 0:384], st2[:, 0:P], wo[:, 3 * j:3 * j + 3, :], start=True, stop=True)
            assert did(mm) == A_MOD
            pe.wait_ge(a_dve, AD_H)
            for t in range(NT):
                mm = pe.transpose(tile(0, t), tok(sq)[:, t, :], ident)
            assert did(mm) == A_T1
            pe.wait_ge(a_act, AA_HT)
            pe.wait_ge(a_dve, AD_MOD)
            pe.wait_ge(in_wa, 32)
            for t in range(NT):
                mm = pe.matmul(ps[:, t // 2, (t % 2) * 256:(t % 2) * 256 + 256], u[:, t * P:t * P + P], w1[:, 0:256], start=True, stop=True)
            assert did(mm) == A_KV
            pe.wait_ge(a_dve, AD_PRE)
            for t in range(NT):
                mm = pe.matmul(tile(0, t), cst[:, C_TRI:C_TRI + P], tok(u)[:, t, :], start=True, stop=(t == 0))
                if t:
                    mm = pe.matmul(tile(0, t), cst[:, C_ONE:C_ONE + P], pre[:, t, :], start=False, stop=True)
            assert did(mm) == A_CUM
            pe.wait_ge(a_dve, AD_N)
            for t in range(NT):
                mm = pe.transpose(tile(4, t), tok(u)[:, t, :], ident)
            assert did(mm) == A_T2
            pe.wait_ge(a_act, AA_NT)
            for t in range(NT):
                mm = pe.matmul(tile(0, t), t1[:, t * P:t * P + P], w1[:, 256:384], start=True, stop=True)
            assert did(mm) == A_WO
            pe.wait_ge(a_dve, AD_H2)
            for t in range(NT):
                mm = pe.transpose(tile(4, t), tok(t1)[:, t, :], ident)
            assert did(mm) == A_T3

            def project(g, before):
                pe.wait_ge(xs_ready, g * 2 + 2)
                pe.wait_ge(x_added, before + FREE)
                pe.wait_ge(rotated, g * 4 + FREE)
                for c, bk in enumerate(QK_BANK + V_BANK):
                    if c == 2:
                        pe.wait_ge(o_normed, before + FREE)
                    if c == 4:
                        pe.wait_ge(v_evac, g * 2 + FREE)
                    pe.matmul(ps[:, bk, :], xs[:, :], wbuf[:, c * 512:c * 512 + 512],
                              start=True, stop=True).then_inc(proj_done, 1)

            def transpose4(bk, src, b, done):
                for j in range(4):
                    mm = pe.transpose(ps[:, bk, j * P:j * P + P], src[:, (4 * b + j) * P:(4 * b + j + 1) * P], ident)
                mm.then_inc(done, 1)

            def transpose_qk(g, projected):
                pe.wait_ge(q_normed, g + 1)
                pe.wait_ge(v_evac, projected * 2 + FREE)
                for b in range(2):
                    transpose4(2 + b, u[:, 0:INNER], b, q_trans)
                pe.wait_ge(k_normed, g + 1 + FREE)
                pe.wait_ge(rotated, projected * 4 - 2 + FREE)
                for b in range(2):
                    transpose4(b, u[:, INNER:2 * INNER], b, k_trans)

            def scores(g, m):
                pe.wait_ge(k_evac, g * 4 + 4)
                pe.wait_ge(q_evac, g * 2 + 2)
                pe.wait_ge(shifted, g + FREE)
                for b in range(2):
                    bk = ps[:, 4 + b, :]
                    pe.matmul(bk, identb[:, :], maskb[:, m, :, :].rearrange("p h n -> p (h n)"), start=True, stop=True)
                    for j in range(4):
                        hp = 4 * b + j
                        for w in range(NW):
                            last = pe.matmul(ps[W * w:W * w + W, 4 + b, j * P:j * P + P], qT[:, hp, W * w:W * w + W],
                                             kT[:, :, hp, W * w:W * w + 2 * W], start=False, stop=True,
                                             skip_group_check=True)
                last.then_inc(scored, 1)

            def transpose_p(g, projected):
                pe.wait_ge(exp_done, g + 1)
                pf = pr[:, :, :].rearrange("p h n -> p (h n)")
                for b in range(2):
                    pe.wait_ge(v_evac, projected * 2 - 1 + b + FREE)
                    transpose4(2 + b, pf, b, p_trans)

            def values(g, projected):
                pe.wait_ge(v_frames, g * 64 + 64 + FREE)
                pe.wait_ge(o_normed, g + FREE)
                for b in range(2):
                    pe.wait_ge(rotated, projected * 4 - 1 + b + FREE)
                    pe.wait_ge(p_evac, g * 2 + 1 + b)
                    for j in range(4):
                        hp = 4 * b + j
                        for w in range(NW):
                            last = pe.matmul(ps[W * w:W * w + W, 6 + b, j * P:j * P + P],
                                             pT[:, hp, W * w:W * w + W], vf[:, :, w, hp * DH:hp * DH + DH],
                                             start=True, stop=True)
                last.then_inc(av_done, 1)

            def transpose_o(g, transposed):
                pe.wait_ge(o_normed, g + 1 + FREE)
                for b in range(2):
                    pe.wait_ge(q_evac, transposed * 2 - 1 + b)
                    transpose4(2 + b, o, b, o_trans)

            def project_o(g, transposed):
                pe.wait_ge(k_evac, transposed * 4 - 2)
                pe.wait_ge(x_added, g + FREE)
                for k in range(HP):
                    pe.wait_ge(o_evac, g * 2 + 1 + k // 4)
                    mm = pe.matmul(ps[:, 0, 0:P], wo[:, k, :], oT[:, k, :], start=(k == 0), stop=(k == HP - 1))
                mm.then_inc(y_done, 1)

            pe.wait_ge(masks_ready, 3)
            with pe.Fori(0, LAYERS) as L:
                pe.wait_ge(in_wqkv, L * 16 + 16)
                pe.wait_ge(in_wo, L * 16 + 16)
                project(L * NT, L * NT)
                project(L * NT + 1, L * NT)
                transpose_qk(L * NT, L * NT + 2)
                scores(L * NT, 1)
                with pe.Fori(0, NT - 2) as t:
                    g = L * NT + t
                    project(g + 2, g)
                    transpose_p(g, g + 3)
                    values(g, g + 3)
                    transpose_qk(g + 1, g + 3)
                    transpose_o(g, g + 2)
                    project_o(g, g + 2)
                    scores(g + 1, 0)
                for t in (NT - 2, NT - 1):
                    g, end = L * NT + t, L * NT + NT
                    transpose_p(g, end)
                    values(g, end)
                    if t < NT - 1:
                        transpose_qk(g + 1, end)
                    transpose_o(g, end)
                    project_o(g, end)
                    if t < NT - 1:
                        scores(g + 1, 0)
                def centre(c):
                    f = L * NC_ + c
                    pe.wait_ge(f_xs, f * 2 + 2)
                    if c >= 2:
                        pe.wait_ge(f_cp, f - 1)
                    pe.matmul(ps[:, c % 2, :], cen, fxs[:, c, :], start=True, stop=True).then_inc(f_cen, 1)

                def variance(c):
                    f = L * NC_ + c
                    pe.wait_ge(f_sq, f + 1)
                    if c >= 2:
                        pe.wait_ge(f_std, f - 1)
                    pe.matmul(ps[:, 2 + c % 2, :], avg, fsq[:, c, :], start=True, stop=True).then_inc(f_var, 1)

                centre(0)
                for c in range(NC_):
                    if c + 1 < NC_:
                        centre(c + 1)
                    variance(c)
                pe.wait_ge(f_cp, L * NC_ + NC_)
                pe.wait_ge(f_std, L * NC_ + NC_)
                pe.wait_ge(in_w12, L * 32 + 32)
                for c in range(NC_):
                    f = L * NC_ + c
                    pe.wait_ge(f_aff, f + 1)
                    for k in range(3):
                        if c:
                            pe.wait_ge(f_gelu, L * (3 * NC_) + 3 * c - 2 + k)
                        pe.matmul(ps[0:KT[k], GATE_BANK[k], :], w1[:, DI + 128 * k:DI + 128 * k + KT[k]], fxs[:, c, :],
                                  start=True, stop=True).then_inc(f_gate, 1)
                        if c:
                            pe.wait_ge(f_ag, L * (3 * NC_) + 3 * c - 2 + k + FREE)
                        pe.matmul(ps[0:KT[k], A_BANK[k], :], w1[:, 128 * k:128 * k + KT[k]], fxs[:, c, :],
                                  start=True, stop=True).then_inc(f_a, 1)
                    if c >= 2:
                        pe.wait_ge(f_x, f - 1 + FREE)
                    for k in range(3):
                        pe.wait_ge(f_ag, L * (3 * NC_) + 3 * c + k + 1 + FREE)
                        mm = pe.matmul(ps[:, 6 + c % 2, :], w2[0:KT[k], k, :], fg[0:KT[k], k, :], start=(k == 0), stop=(k == 2))
                    mm.then_inc(f_y, 1)
            pe.wait_ge(f_x, LAYERS * NC_ + FREE)
            for t in range(NT):
                mm = pe.transpose(tile(0, t), xT[:, 1 + t * P:1 + t * P + P], ident)
            assert did(mm) == C_T

        @block.vector
        def _(v):
            step = [0]

            def did(ins):
                step[0] += 1
                ins.then_inc(a_dve, 1)
                v.wait_ge(a_dve, step[0])
                return step[0]

            def rsqrt(y, s, a):
                yield lambda: v.tensor_scalar(a.bitcast(I32), s.bitcast(I32), 1, None, ALU.arith_shift_right)
                yield lambda: v.tensor_scalar(y.bitcast(I32), a.bitcast(I32), -1.0, float(RSQRT_MAGIC), ALU.mult, ALU.add)
                for _ in range(NEWTON):
                    yield lambda: v.scalar_tensor_tensor(a, y, -0.5, y, ALU.mult, ALU.mult)
                    yield lambda: v.tensor_tensor(a, a, s, ALU.mult)
                    yield lambda: v.scalar_tensor_tensor(y, a, 1.5, y, ALU.add, ALU.mult)

            def centre(dst, src):
                do = did
                do(v.tensor_reduce(st[:, 0:NT], src, AX, ALU.add))
                do(v.tensor_scalar(st[:, 0:NT], st[:, 0:NT], -1.0 / D, None, ALU.mult))
                return do(v.tensor_tensor(dst, src, st[:, 0:NT].unsqueeze(2).broadcast_to([P, NT, D]), ALU.add))

            def normalise(dst, src, square, squared_step):
                v.wait_ge(a_act, squared_step)
                did(v.tensor_reduce(st[:, 0:NT], square, AX, ALU.add))
                did(v.tensor_scalar(st[:, 0:NT], st[:, 0:NT], 1.0 / D, LN_EPS, ALU.mult, ALU.add))
                for newton in rsqrt(st2[:, 0:NT], st[:, 0:NT], st3[:, 0:NT]):
                    did(newton())
                return did(v.tensor_tensor(dst, src, st2[:, 0:NT].unsqueeze(2).broadcast_to([P, NT, D]), ALU.mult))

            def over_tiles(r):
                return r.unsqueeze(1).broadcast_to([P, NT, D])

            def quat_mul(dst, a, b, tmp, conj):
                sg = lambda i, c: SIGN[i][c] * (-1 if conj and PERM[i][c] else 1)
                for c in range(4):
                    did(v.scalar_tensor_tensor(dst[:, :, c], a[:, :, 0], float(sg(0, c)), b[:, :, c], ALU.mult, ALU.mult))
                for i in range(1, 4):
                    for c in range(4):
                        did(v.tensor_tensor(tmp, a[:, :, i], b[:, :, PERM[i][c]], ALU.mult))
                        n = did(v.tensor_tensor(dst[:, :, c], dst[:, :, c], tmp, ALU.add if sg(i, c) > 0 else ALU.subtract))
                return n

            quats = lambda b: b[:, 0:N].rearrange("p (q c) -> p q c", c=4)

            v.wait_ge(a_act, AA_EXPC)
            did(v.tensor_scalar(st[:, 2:3], st[:, 1:2], 1.0, None, ALU.add))
            did(v.reciprocal(st[:, 3:4], st[:, 2:3]))
            did(v.tensor_tensor(st[:, 4:5], st[:, 3:4], st[:, 0:1], ALU.mult))
            v.wait_ge(in_cst, 16)
            assert did(v.tensor_scalar(st2[:, 0:P], cst[:, C_ONE:C_ONE + P], st[:, 4:5], None, ALU.mult)) == AD_SILU
            v.wait_ge(a_pe, A_MOD)
            for j in range(2):
                did(v.tensor_copy(mod[:, 384 * j:384 * j + 384], ps[:, 6 + j, 0:384]))
            sa, ca, ga, sb_, cb, gb = (mod[:, D * j:D * j + D] for j in range(6))
            for m in (ca, cb):
                did(v.tensor_scalar(m, m, 1.0, None, ALU.add))
            for m in (ga, gb):
                did(v.tensor_scalar(st3[:, 0:D], m, 0.0, None, ALU.is_ge))
                did(v.tensor_scalar(st3[:, 0:D], st3[:, 0:D], 2.0, -1.0, ALU.mult, ALU.add))
                did(v.tensor_scalar(st3[:, D:2 * D], m, -1.0, 0.25, ALU.mult, ALU.max))
                did(v.tensor_tensor(m, m, st3[:, D:2 * D], ALU.max))
                n = did(v.tensor_tensor(m, m, st3[:, 0:D], ALU.mult))
            assert n == AD_MOD, n
            v.wait_ge(in_x, 16)
            n = centre(tok(t1), x1[:, :, :])
            assert n == AD_XC1, n
            normalise(tok(t1), tok(t1), tok(t2), AA_SQ1)
            did(v.tensor_tensor(tok(t1), tok(t1), over_tiles(ca), ALU.mult))
            n = did(v.tensor_tensor(tok(sq), tok(t1), over_tiles(sa), ALU.add))
            assert n == AD_H, n
            v.wait_ge(a_pe, A_KV)
            did(v.tensor_copy(h_keep, sq[:, 0:N]))
            kv = ps[:, :, :].rearrange("p b (t n) -> p (b t) n", n=256)
            did(v.tensor_tensor(tok(t2), kv[:, :, D:2 * D], over_tiles(row[:, R_BKV + D:R_BKV + 2 * D]), ALU.add))
            n = did(v.tensor_tensor(tok(t1), kv[:, :, 0:D], over_tiles(row[:, R_BKV:R_BKV + D]), ALU.add))
            assert n == AD_KV, n
            v.wait_ge(a_act, AA_KSQ)
            did(v.tensor_reduce(st[:, :], quats(sq), AX, ALU.add))
            did(v.tensor_scalar(st[:, :], st[:, :], NORM_GUARD, None, ALU.max))
            for newton in rsqrt(st2[:, :], st[:, :], st3[:, :]):
                did(newton())
            did(v.tensor_tensor(quats(t1), quats(t1), st2[:, :].unsqueeze(2).broadcast_to([P, NQ, 4]), ALU.mult))
            quat_mul(quats(u), quats(t2), quats(t1), st[:, :], False)
            n = did(v.tensor_copy(pre[:, 1, :], tok(u)[:, 0, :]))
            for t in range(2, NT):
                n = did(v.tensor_tensor(pre[:, t, :], pre[:, t - 1, :], tok(u)[:, t - 1, :], ALU.add))
            assert n == AD_PRE, n
            v.wait_ge(a_act, AA_MEM)
            quat_mul(quats(sq), quats(t2), quats(t1), st[:, :], True)
            did(v.tensor_tensor(tok(sq), tok(sq), cst[:, C_RSQ:C_RSQ + NT].unsqueeze(2).broadcast_to([P, NT, D]), ALU.mult))
            n = centre(tok(u), tok(sq))
            assert n == AD_XC2, n
            normalise(tok(u), tok(u), tok(t2), AA_SQ2)
            did(v.tensor_tensor(tok(u), tok(u), over_tiles(row[:, R_G:R_G + D]), ALU.mult))
            n = did(v.tensor_tensor(tok(u), tok(u), over_tiles(row[:, R_B:R_B + D]), ALU.add))
            assert n == AD_N, n
            v.wait_ge(a_pe, A_WO)
            y = ps[:, 0:4, :].rearrange("p b (t d) -> p (b t) d", d=D)
            did(v.tensor_tensor(tok(t1), y, over_tiles(row[:, R_BO:R_BO + D]), ALU.add))
            did(v.tensor_tensor(t1[:, 0:N], t1[:, 0:N], h_keep, ALU.add))
            did(v.tensor_tensor(tok(t1), tok(t1), over_tiles(ga), ALU.mult))
            did(v.tensor_tensor(x1[:, :, :], x1[:, :, :], tok(t1), ALU.add))
            n = centre(tok(t1), x1[:, :, :])
            assert n == AD_XC3, n
            normalise(tok(t1), tok(t1), tok(t2), AA_SQ3)
            did(v.tensor_tensor(tok(t1), tok(t1), over_tiles(cb), ALU.mult))
            n = did(v.tensor_tensor(tok(t1), tok(t1), over_tiles(sb_), ALU.add))
            assert n == AD_H2, n

            def stage(t, g):
                v.wait_ge(proj_done, g * 6 + FREE)
                v.tensor_scalar(xs[0:64, :], xT[0:64, bass.ds(t * P + 1, P)], 1.0, None, ALU.mult).then_inc(xs_ready, 1)
                v.tensor_scalar(xs[64:P, :], xT[64:P, bass.ds(t * P, P)], 1.0, None, ALU.mult).then_inc(xs_ready, 1)

            def rotate(t, g):
                v.wait_ge(added, g * 4 + FREE)
                for c in range(4):
                    v.wait_ge(squared, g * 4 + c + 1)
                    q = ps[:, QK_BANK[c], :].rearrange("p (h d) -> p h d", d=DH).unsqueeze(1).broadcast_to([P, 2, 8, DH])
                    j = 2 * (c // 2)
                    cs = tabl[:, bass.ds(t, 1), j * DH:(j + 2) * DH].rearrange("p a (s d) -> p s a d", d=DH).broadcast_to([P, 2, 8, DH])
                    v.tensor_tensor(tr[:, c, :, :].rearrange("p s (h d) -> p s h d", d=DH), q, cs, ALU.mult).then_inc(rotated, 1)

            def sum_squares(g):
                v.wait_ge(squared, g * 4 + 4)
                v.tensor_reduce(ss[:, :], sq[:, :].rearrange("p (h d) -> p h d", d=DH), AX, ALU.add).then_inc(sq_summed, 1)

            def inv_norms(g):
                v.wait_ge(sq_summed, g + 1 + FREE)
                v.wait_ge(k_normed, g + FREE)
                v.tensor_scalar(ss[:, :], ss[:, :], NORM_GUARD, None, ALU.max).then_inc(link, 1)
                for n, newton in enumerate(rsqrt(rn[:, :], ss[:, :], ra[:, :])):
                    v.wait_ge(link, g * NORM_LINKS + n + 1)
                    newton().then_inc(link, 1)

            def shift_by_max(g):
                v.wait_ge(scored, g + 1 + FREE)
                v.wait_ge(p_trans, g * 2 + FREE)
                s = ps[:, 4:6, :].rearrange("p b (h n) -> p (b h) n", n=2 * W)
                v.tensor_reduce(mx[:, :], s, AX, ALU.max).then_inc(max_ready, 1)
                v.wait_ge(max_ready, g + 1)
                v.tensor_tensor(pr[:, :, :], s, mx[:, :].unsqueeze(2).broadcast_to([P, H, 2 * W]), ALU.subtract).then_inc(shifted, 1)

            def inv_sums(g):
                v.wait_ge(exp_done, g + 1)
                v.tensor_reduce(rs[:, :], pr[:, :, :], AX, ALU.add).then_inc(sum_ready, 1)
                v.wait_ge(sum_ready, g + 1)
                v.reciprocal(ri[:, :], rs[:, :]).then_inc(rsum_ready, 1)

            def output(g):
                v.wait_ge(rsum_ready, g + 1)
                v.wait_ge(av_done, g + 1 + FREE)
                v.wait_ge(o_trans, g * 2 + FREE)
                a = ps[:, 6:8, :].rearrange("p b (h n) -> p (b h) n", n=DH)
                v.tensor_tensor(o.rearrange("p (h n) -> p h n", n=DH), a,
                                ri[:, :].unsqueeze(2).broadcast_to([P, H, DH]), ALU.mult).then_inc(o_normed, 1)

            def add_x(t, g):
                v.wait_ge(y_done, g + 1 + FREE)
                xt = xT[:, bass.ds(t * P + 1, P)]
                v.tensor_tensor(xt, ps[:, 0, 0:P], xt, ALU.add).then_inc(x_added, 1)

            v.wait_ge(in_prm, 16)
            v.wait_ge(a_act, A_XT)
            with v.Fori(0, LAYERS) as L:
                v.wait_ge(f_x, L * NC_ + FREE)
                v.tensor_copy(pl[:, :], prm[:, bass.ds(L, 1), :].rearrange("p a n -> p (a n)")).then_inc(f_prm, 1)
                stage(0, L * NT)
                v.wait_ge(tabs_ready, L + 1)
                for t in range(2):
                    if t:
                        stage(t, L * NT + t)
                    rotate(t, L * NT + t)
                    sum_squares(L * NT + t)
                    inv_norms(L * NT + t)
                with v.Fori(0, NT - 2) as t:
                    g = L * NT + t
                    stage(t + 2, g + 2)
                    shift_by_max(g)
                    rotate(t + 2, g + 2)
                    inv_sums(g)
                    output(g)
                    sum_squares(g + 2)
                    inv_norms(g + 2)
                    add_x(t, g)
                for t in (NT - 2, NT - 1):
                    g = L * NT + t
                    shift_by_max(g)
                    inv_sums(g)
                    output(g)
                    add_x(t, g)
                v.wait_ge(x_added, L * NT + NT + FREE)
                for c in range(NC_):
                    v.tensor_copy(fxs[0:64, c, :], xT[0:64, 1 + c * CH:1 + c * CH + CH]).then_inc(f_xs, 1)
                    v.tensor_copy(fxs[64:P, c, :], xT[64:P, c * CH:c * CH + CH]).then_inc(f_xs, 1)
                for c in range(NC_):
                    f = L * NC_ + c
                    v.wait_ge(f_sq, f + 1)
                    v.tensor_copy(fxc[:, c, :], ps[:, c % 2, :]).then_inc(f_cp, 1)
                def normalise_chunk(c):
                    f = L * NC_ + c
                    v.wait_ge(f_std, f + 1)
                    v.reciprocal(fsq[:, c, :], fsq[:, c, :]).then_inc(f_rstd, 1)
                    v.wait_ge(f_rstd, f + 1)
                    v.tensor_tensor(fxs[:, c, :], fxc[:, c, :], fsq[:, c, :], ALU.mult).then_inc(f_xn, 1)
                    v.wait_ge(f_xn, f + 1)
                    v.wait_ge(f_prm, L + 1)
                    v.tensor_scalar(fxs[:, c, :], fxs[:, c, :], pl[:, L_G:L_G + 1], pl[:, L_B:L_B + 1], ALU.mult, ALU.add).then_inc(f_aff, 1)

                normalise_chunk(0)
                for c in range(NC_):
                    f = L * NC_ + c
                    if c + 1 < NC_:
                        normalise_chunk(c + 1)
                    for k in range(3):
                        i = L * (3 * NC_) + 3 * c + k + 1
                        v.wait_ge(f_a, i)
                        v.wait_ge(f_gelu, i)
                        g_ = fg[0:KT[k], k, :]
                        v.scalar_tensor_tensor(g_, ps[0:KT[k], A_BANK[k], :], pl[0:KT[k], L_BA + k:L_BA + k + 1], g_,
                                               ALU.add, ALU.mult).then_inc(f_ag, 1)
                    v.wait_ge(f_y, f + 1 + FREE)
                    xt = xT[:, 1 + c * CH:1 + c * CH + CH]
                    v.scalar_tensor_tensor(xt, ps[:, 6 + c % 2, :], pl[:, L_B2:L_B2 + 1], xt, ALU.add, ALU.add).then_inc(f_x, 1)
            v.wait_ge(a_pe, C_T)
            y = ps[:, 0:4, :].rearrange("p b (t d) -> p (b t) d", d=D)
            did(v.tensor_tensor(tok(t1), y, over_tiles(gb), ALU.mult))
            n = did(v.tensor_tensor(x1[:, :, :], x1[:, :, :], tok(t1), ALU.add))
            assert n == C_OUT, n




def rotary_tables():
    f = np.float32
    half = np.arange(0, DH, 2, dtype=f)
    inv_freq = (f(1) / np.power(f(10000), half / f(DH))).astype(f)
    pos = np.arange(N, dtype=f)
    freqs = (pos[:, None] * inv_freq[None, :]).astype(f).astype(np.float64)
    base = ((half + f(0.4 * DH)) / f(1.4 * DH)).astype(np.float64)
    scale = base[None, :] ** ((np.arange(N) % P - P // 2) / (W // 2))[:, None]
    cos, sin = np.cos(freqs), np.sin(freqs)
    parts = []
    for s in (scale, 1.0 / scale):
        parts += [cos * s, cos * s, sin * s, -sin * s]
    carry = np.tile(base ** (P / (W // 2)), P // len(base))
    return np.concatenate(parts, 1).astype(f), carry.astype(f)


def constants(carry):
    c = np.zeros((P, C_END), np.float32)
    i = np.arange(P)
    c[:, C_ID:C_ID + P] = np.eye(P)
    c[:, C_TRI:C_TRI + P] = i[:, None] <= i[None, :]
    c[:, C_ONE:C_ONE + P] = 1
    c[:, C_AVG:C_AVG + P] = 1 / D
    c[:, C_CEN:C_CEN + P] = np.eye(P) - 1 / D
    q, k = i[:, None] % W, np.arange(2 * W)[None, :]
    seen = (k >= q) & (k <= q + W)
    c[:, C_MASK:C_MASK + 2 * W] = np.where(seen, 0, MASKED)
    c[:, C_MASK0:C_MASK0 + 2 * W] = np.where(seen & ((i[:, None] >= W) | (k >= W)), 0, MASKED)
    c[:, C_KS] = carry
    c[:, C_RSQ:C_RSQ + NT] = 1 / np.sqrt(np.arange(1, N + 1).reshape(NT, P).T)
    c[:, C_EPS] = LN_EPS
    return c


def kernel(**inputs):
    import concourse.bacc as bacc
    from concourse.bass_utils import run_bass_kernel_spmd

    a = {k: np.asarray(v) for k, v in inputs.items()}
    f = np.float32
    tab, carry = rotary_tables()
    wqkv = a["L0_ffn_Wqkv"]
    v = wqkv[:, :, 2 * INNER:].reshape(LAYERS, D, HP, 2, DH).transpose(0, 1, 3, 2, 4).reshape(LAYERS, D, INNER)
    qs, ks = a["L0_ffn_q_scale"], a["L0_ffn_k_scale"]
    w2 = np.zeros((LAYERS, 3 * P, D), f)
    w2[:, :DI] = a["L0_ffn_W2"]
    prm = np.zeros((P, LAYERS, L_END), f)
    prm[:, :, L_G], prm[:, :, L_B], prm[:, :, L_B2] = a["L0_ffn_ln_g"].T, a["L0_ffn_ln_b"].T, a["L0_ffn_b2"].T
    for k, n in enumerate(KT):
        prm[:n, :, L_BA + k] = a["L0_ffn_b1"][:, P * k:P * k + n].T
        prm[:n, :, L_BG + k] = a["L0_ffn_b1"][:, DI + P * k:DI + P * k + n].T
    arrays = {
        "x": a["L0_attn_x"][0],
        "cst": constants(carry),
        "row": np.concatenate([a["L0_attn_bk"], a["L0_attn_bv"], a["L0_attn_ln_g"], a["L0_attn_ln_b"], a["L0_attn_bo"]]),
        "c": a["L0_c"].reshape(D, 1),
        "wmod": a["L0_wmod"],
        "wkv": np.concatenate([a["L0_attn_Wk"].T, a["L0_attn_Wv"].T], 1),
        "woa": a["L0_attn_Wo"].T,
        "tab": tab,
        "scl": np.concatenate([qs, qs, ks, ks], 1),
        "wqkv": np.concatenate([wqkv[:, :, :2 * INNER], v], 2).reshape(LAYERS * D, 3 * INNER),
        "wo": a["L0_ffn_Wo"].reshape(LAYERS, HP, P, D).transpose(0, 2, 1, 3).reshape(LAYERS * P, HP * D),
        "w1": a["L0_ffn_W1"].reshape(LAYERS * D, 2 * DI),
        "w2": w2.reshape(LAYERS, 3, P, D).transpose(0, 2, 1, 3).reshape(LAYERS * P, 3 * D),
        "prm": prm,
    }
    arrays = {f"in_{k}": np.ascontiguousarray(x) for k, x in arrays.items()}
    nc = bacc.Bacc("TRN2", target_bir_lowering=False, num_devices=1)
    args = [nc.dram_tensor(k, x.shape, mybir.dt.from_np(x.dtype), kind="ExternalInput").ap() for k, x in arrays.items()]
    out = nc.dram_tensor("out", [N, D], F32, kind="ExternalOutput").ap()
    program(nc, *args, out)
    r = run_bass_kernel_spmd(nc, [arrays], core_ids=[0])
    return r.results[0]["out"].reshape(1, N, D)
```

```python
import numpy as np
import concourse.bass as bass
from concourse import mybir
from contextlib import ExitStack

F32 = mybir.dt.float32
BF16 = mybir.dt.bfloat16
I32 = mybir.dt.int32
F32R = mybir.dt.float32r
ALU = mybir.AluOpType
ACT = mybir.ActivationFunctionType
AX = mybir.AxisListType.X

N, D = 2048, 128
P = 128
NT = N // P
LAYERS, H, DH, W = 6, 16, 64, 32
HP = H // 2
NW = P // W
INNER = H * DH
DI = 341
CH = 512
NC_ = N // CH
NQ = N * D // (P * 4)
PARTS = [(0, NT - CH // P), (NT - CH // P, NT)]
KT = [128, 128, DI - 256]
LN_EPS = 1e-5
NORM_GUARD = 1e-24
MASKED = -1e30
RSQRT_MAGIC = 0x5F3759DF

C_ID, C_TRI, C_ONE, C_AVG, C_CEN, C_MASK, C_MASK0 = 0, 128, 256, 384, 512, 640, 704
C_KS, C_RSQ, C_EPS, C_END = 768, 769, 785, 786
R_BKV, R_BO, R_END = 0, 256, 384
V_C, V_G, V_B, V_SA, V_CA, V_SB, V_CB, V_END = range(8)
MOD_ORDER = [0, 1, 3, 4]
L_G, L_B, L_B2, L_BA, L_BG, L_END = 0, 1, 2, 3, 6, 9

Y_BANK = 3
CENTRE_BANK, STD_BANK = [6, 7, 1, 1], [6, 7, 6, 2]
VAR_BANK, ROW_BANK, BIAS_BANK = [0, 2], [3, 2], 0
STAT_ROW = 128
GATE_BANK = lambda c, k: 0 if c == 0 and k != 1 else 4
A_BANK = lambda c, k: GATE_BANK(c, k) + 1
BACK_BANK = [0, 1, 6, 7]
QK_BANK, V_BANK = [6, 7, 0, 1], [2, 3]
AD_SILU, AD_XC1, AD_MOD, AD_N1, AD_K, AD_KN, AD_Q1, AD_PRE, AD_Q2, AD_XC2, AD_N2, AD_X1, AD_XC3, AD_N3, C_OUT = \
    5, 7, 19, 36, 40, 57, 78, 79, 114, 117, 137, 141, 151, 171, 176
AA_EXPC, AA_SQ1, AA_HT, AA_V, AA_MEM, AA_SQ2, AA_NT, AA_SQ3, A_XT = 1, 2, 6, 10, 18, 22, 26, 30, 34
A_MOD, A_T1, A_KV, A_CUM, A_T2, A_WO, A_T3, C_T = 1, 2, 6, 10, 14, 18, 22, 26
AP_V, AP_Q1, AP_Q2 = 1, 8, 15
FREE = 1
NEWTON = 3
NORM_LINKS = 1 + 2 + 3 * NEWTON
EARLY = NORM_LINKS - 4

PERM = [[0, 1, 2, 3], [1, 0, 3, 2], [2, 3, 0, 1], [3, 2, 1, 0]]
SIGN = [[1, 1, 1, 1], [-1, 1, -1, 1], [-1, 1, 1, -1], [-1, -1, 1, 1]]


def program(nc, x_d, cst_d, row_d, c_d, wmod_d, wkv_d, woa_d, tab_d, scl_d, wqkv_d, wo_d, w1_d, w2_d, prm_d,
            out_d):
    ctx = ExitStack()
    with ctx:
        def sb(name, shape, dt=F32):
            return ctx.enter_context(nc.sbuf_tensor(name, shape, dt))

        def sem(name):
            return ctx.enter_context(nc.semaphore(name))

        cst = sb("cst", [P, C_END])
        row = sb("row", [P, R_END])
        maskb = sb("maskb", [P, 2, 8, 2 * W], BF16)
        identb = sb("identb", [P, P], BF16)
        mod = sb("mod", [P, 2 * D])
        vec = sb("vec", [P, V_END])
        x1 = sb("x1", [P, NT, D])
        xT = sb("xT", [P, 1 + N])
        whi = sb("whi", [P, 3 * INNER], F32R)
        wlo = sb("wlo", [P, 3 * INNER], F32R)
        wo = sb("wo", [P, HP, D])
        w1 = sb("w1", [P, 2 * DI])
        w2 = sb("w2", [P, 3, D])
        prm = sb("prm", [P, LAYERS, L_END])
        pl = sb("pl", [P, L_END])
        scl = sb("scl", [P, LAYERS, 4 * DH])
        tab = sb("tab", [P, NT, 4 * DH])
        tabl = sb("tabl", [P, NT, 4 * DH])
        xs = sb("xs", [P, 2, P], F32R)
        sq = sb("sq", [P, 2 * INNER])
        tr = sb("tr", [P, 4, 2, 512])
        t1, t2 = (tr[:, 2 * j:2 * j + 2, :, :].rearrange("p a b n -> p (a b n)") for j in range(2))
        u = sb("u", [P, 2 * INNER])
        ss = sb("ss", [P, 2 * H])
        rn = sb("rn", [P, 2 * H])
        ra = sb("ra", [P, 2 * H])
        vs = sb("vs", [P, 2, HP * DH])
        vf = sb("vf", [P, 2, NW, HP * DH])
        qT = sb("qT", [P, HP, P])
        kT = sb("kT", [P, 2, HP, W + P])
        pr = sb("pr", [P, H, 2 * W])
        mx = sb("mx", [P, H])
        rs = sb("rs", [P, H])
        ri = sb("ri", [P, H])
        pT = sb("pT", [P, HP, P])
        od = sb("od", [P, 2 * INNER])
        o = od[:, 0:INNER]
        oT = od[:, INNER:2 * INNER].rearrange("p (k n) -> p k n", n=P)
        fg = sb("fg", [P, 3, CH])
        st, st2, st3 = (fg[:, j, :] for j in range(3))
        fxn = sb("fxn", [P, NC_, CH])
        fvar, frs, fra = (sb(n, [P, NT]) for n in ("fvar", "frs", "fra"))
        frow = row[:, 0:2 * P].rearrange("p (a n) -> p a n", n=P)
        b1 = sb("b1", [P, 2, 3])
        wland = tabl[:, :, :].rearrange("p t c -> p (t c)")[:, 0:3 * INNER]
        tok = lambda b: b[:, 0:N].rearrange("p (t d) -> p t d", d=D)
        hT = od[:, :]
        pre = xT[:, 1:1 + N].rearrange("p (t d) -> p t d", d=D)
        ps = ctx.enter_context(nc.psum_tensor("ps", [P, 8, 512], F32))

        v_scr = nc.dram_tensor("v_scratch", [W + N, 2 * HP * DH], F32, kind="Internal").ap()

        in_x, in_cst, in_vec, in_wa = sem("in_x"), sem("in_cst"), sem("in_vec"), sem("in_wa")
        w_high, w_low = sem("w_high"), sem("w_low")
        in_tab, in_prm, zero_row = sem("in_tab"), sem("in_prm"), sem("zero_row")
        in_wqkv, in_wo, in_w12 = sem("in_wqkv"), sem("in_wo"), sem("in_w12")
        cleared, tabs_ready, masks_ready = sem("cleared"), sem("tabs_ready"), sem("masks_ready")
        a_dve, a_act, a_pe, a_pool = sem("a_dve"), sem("a_act"), sem("a_pe"), sem("a_pool")
        xs_ready, qk_projected, v_projected, v_evac = sem("xs_ready"), sem("qk_projected"), sem("v_projected"), sem("v_evac")
        v_stored, v_frames = sem("v_stored"), sem("v_frames")
        squared, rotated, added, sq_summed, link, folded = sem("squared"), sem("rotated"), sem("added"), sem("sq_summed"), sem("link"), sem("folded")
        q_normed, k_normed, q_trans, k_trans = sem("q_normed"), sem("k_normed"), sem("q_trans"), sem("k_trans")
        q_evac, k_evac, k_carried = sem("q_evac"), sem("k_evac"), sem("k_carried")
        scored, max_ready, shifted, exp_done = sem("scored"), sem("max_ready"), sem("shifted"), sem("exp_done")
        sum_ready, rsum_ready = sem("sum_ready"), sem("rsum_ready")
        p_trans, p_evac, av_done, o_normed = sem("p_trans"), sem("p_evac"), sem("av_done"), sem("o_normed")
        o_trans, o_evac, y_done, x_added = sem("o_trans"), sem("o_evac"), sem("y_done"), sem("x_added")
        f_xs, f_cen, f_sq, f_var, f_cp = sem("f_xs"), sem("f_cen"), sem("f_sq"), sem("f_var"), sem("f_cp")
        f_link, f_bsum, f_bias, f_rows, f_rowcopy = sem("f_link"), sem("f_bsum"), sem("f_bias"), sem("f_rows"), sem("f_rowcopy")
        f_std, f_bc, f_xn, f_prm = sem("f_std"), sem("f_bc"), sem("f_xn"), sem("f_prm")
        f_gate, f_a, f_gelu, f_ag, f_y, f_x = sem("f_gate"), sem("f_a"), sem("f_gelu"), sem("f_ag"), sem("f_y"), sem("f_x")
        out_done = sem("out_done")

        ident = cst[:, C_ID:C_ID + P]
        block = ctx.enter_context(nc.Block())

        fxs = sq[:, 0:N].rearrange("p (c n) -> p c n", n=CH)
        fsq = t1[:, 0:N].rearrange("p (c n) -> p c n", n=CH)
        avg = cst[:, C_AVG:C_AVG + P]
        cen = cst[:, C_CEN:C_CEN + P]

        kv_bank = lambda b: ps[:, 2 * b:2 * b + 2, :].rearrange("p b (t n) -> p (b t) n", n=256)
        quats = lambda b: b[:, 0:N].rearrange("p (q c) -> p q c", c=4)

        def quat_terms(i, c, conj):
            return SIGN[i][c] * (-1 if conj and PERM[i][c] else 1), PERM[i][c]

        @block.sync
        def _(sp):
            for s in (v_evac, k_normed, v_frames, av_done, y_done, qk_projected, v_projected, k_trans, scored, rotated, v_stored, sq_summed,
                      f_gelu, f_ag, f_y, shifted, x_added, o_normed, added, p_trans, o_trans, f_x):
                sp.sem_inc(s, FREE)
            sp.dma_start(x1[:, :, :], x_d.rearrange("(t p) d -> p t d", p=P)).then_inc(in_x, 16)
            sp.dma_start(cst[:, :], cst_d).then_inc(in_cst, 16)
            sp.dma_start(vec[:, 0:3], c_d).then_inc(in_vec, 16)
            sp.dma_start(wo[:, 0:6, :], wmod_d.rearrange("p (a d) -> p a d", d=D)).then_inc(in_vec, 16)
            sp.dma_start(row[:, :], row_d.partition_broadcast(P)).then_inc(in_vec, 16)
            sp.dma_start(w1[:, 0:256], wkv_d).then_inc(in_wa, 16)
            sp.dma_start(w1[:, 256:384], woa_d).then_inc(in_wa, 16)
            sp.dma_start(scl[:, :, :], scl_d.partition_broadcast(P)).then_inc(in_tab, 16)
            sp.dma_start(tab[:, :, :], tab_d.rearrange("(t p) c -> p t c", p=P)).then_inc(in_tab, 16)
            sp.dma_start(prm[:, :, :], prm_d).then_inc(in_prm, 16)
            sp.wait_ge(cleared, 1)
            sp.dma_start(v_scr[0:W, :], vf[0:W, 0, 0:2, :].rearrange("p w n -> p (w n)")).then_inc(zero_row, 16)
            sp.wait_ge(zero_row, 16)
            sp.wait_ge(a_pe, A_MOD)
            snap = lambda x: x if isinstance(x, int) else sp.snap(x)

            def load_attention(L):
                rows, n_rot, n_y = (snap(x) for x in (L * P, L * (4 * NT) + FREE, L * NT + FREE))
                sp.wait_ge(rotated, n_rot)
                sp.dma_start(wland, wqkv_d[bass.ds(rows, P), :]).then_inc(in_wqkv, 16)
                sp.wait_ge(y_done, n_y)
                sp.dma_start(wo[:, :, :], wo_d[bass.ds(rows, P), :].rearrange("p (k d) -> p k d", d=D)).then_inc(in_wo, 16)

            def load_ffn(L):
                rows, n_f = snap(L * P), snap(L * NC_ + FREE)
                sp.wait_ge(f_y, n_f)
                sp.dma_start(w1[:, :], w1_d[bass.ds(rows, P), :]).then_inc(in_w12, 16)
                sp.dma_start(w2[:, :, :], w2_d[bass.ds(rows, P), :].rearrange("p (k d) -> p k d", d=D)).then_inc(in_w12, 16)

            def move_v(t, g):
                even, odd, n_v, n_fr, n_st, n_av = (snap(x) for x in (t * P, t * P + W, g * 2 + 2 + FREE, g * 64 + FREE, g * 16 + 16 + FREE, g * 2 + FREE))
                sp.wait_ge(v_frames, n_fr)
                sp.wait_ge(v_evac, n_v)
                sp.dma_start(v_scr[bass.ds(odd, P), :], vs[:, :, :].rearrange("p a n -> p (a n)")).then_inc(v_stored, 16)
                sp.wait_ge(av_done, n_av)
                sp.wait_ge(v_stored, n_st)
                for a in range(2):
                    for w, first in enumerate((even, odd)):
                        src = v_scr[bass.ds(first, P), a * HP * DH:(a + 1) * HP * DH]
                        sp.dma_start(vf[DH * a:DH * a + DH, a, w:NW:2, :],
                                     src.rearrange("(w p) n -> p w n", p=2 * W)).then_inc(v_frames, 16)

            load_attention(0)
            sp.wait_ge(a_pe, A_WO + 3)
            def layer(L):
                move_v(0, L * NT)
                load_ffn(L)
                with sp.Fori(1, NT) as t:
                    move_v(t, L * NT + t)

            with sp.Fori(0, LAYERS - 1) as L:
                layer(L)
                load_attention(L + 1)
            layer(LAYERS - 1)
            for b in range(4):
                sp.wait_ge(a_dve, C_OUT + 2 * b)
                sp.dma_start(out_d.rearrange("(t p) d -> p t d", p=P)[:, 4 * b:4 * b + 4, :], x1[:, 4 * b:4 * b + 4, :]).then_inc(out_done, 16)
            sp.wait_ge(out_done, 64)
            sp.wait_ge(v_stored, LAYERS * NT * 16 + FREE)
            sp.wait_ge(v_frames, LAYERS * NT * 64 + FREE)

        @block.gpsimd
        def _(pool):
            pool.memset(vf[:, :, :, :], 0.0).then_inc(cleared, 1)
            pool.memset(kT[:, :, :, :], 0.0).then_inc(cleared, 1)
            pool.memset(xT[:, 0:1], 0.0).then_inc(cleared, 1)
            pool.wait_ge(in_cst, 16)
            pool.tensor_copy(identb[:, :], ident).then_inc(masks_ready, 1)
            for m, c in enumerate((C_MASK, C_MASK0)):
                pool.tensor_copy(maskb[:, m, :, :], cst[:, c:c + 2 * W].unsqueeze(1).broadcast_to([P, 8, 2 * W])).then_inc(masks_ready, 1)
            def finish_qk(g):
                sh = sq[:, :].rearrange("p (h s d) -> p h s d", s=2, d=DH // 2)
                pool.wait_ge(squared, g * 4 + 4)
                pool.tensor_tensor(sh[:, :, 0, :], sh[:, :, 0, :], sh[:, :, 1, :], ALU.add).then_inc(folded, 1)
                pool.wait_ge(k_trans, g * 2 + FREE)
                uh = u[:, :].rearrange("p (j c h d) -> p j c h d", j=2, c=2, d=DH)
                th = tr[:, :, :, :].rearrange("p (j c) s (h d) -> p j c s h d", j=2, d=DH)
                for j in range(2):
                    pool.wait_ge(rotated, g * 4 + 2 * j + 2 + FREE)
                    for x in range(2):
                        lo, hi = slice(32 * x, 32 * x + 32), slice(32 - 32 * x, 64 - 32 * x)
                        pool.tensor_tensor(uh[:, j, :, :, lo], th[:, j, :, 0, :, lo], th[:, j, :, 1, :, hi], ALU.add).then_inc(added, 1)
                pool.wait_ge(link, g * NORM_LINKS + NORM_LINKS)
                for j, done in enumerate((q_normed, k_normed)):
                    pool.wait_ge(added, g * 4 + 2 * j + 2 + FREE)
                    x = u[:, j * INNER:(j + 1) * INNER].rearrange("p (h d) -> p h d", d=DH)
                    pool.tensor_tensor(x, x, rn[:, j * H:(j + 1) * H].unsqueeze(2).broadcast_to([P, H, DH]), ALU.mult).then_inc(done, 1)

            step = [0]

            def did(ins):
                step[0] += 1
                ins.then_inc(a_pool, 1)
                pool.wait_ge(a_pool, step[0])
                return step[0]

            def quat_component(dst, a, b, c, conj):
                tmp = pr[:, 0:8, :].rearrange("p h n -> p (h n)")
                s = quat_terms(0, c, conj)[0]
                did(pool.tensor_tensor(dst[:, :, c], a[:, :, 0], b[:, :, quat_terms(0, c, conj)[1]], ALU.mult))
                for i in range(1, 4):
                    s_i, k = quat_terms(i, c, conj)
                    did(pool.tensor_tensor(tmp, a[:, :, i], b[:, :, k], ALU.mult))
                    if s < 0 and s_i > 0:
                        n, s = did(pool.tensor_tensor(dst[:, :, c], tmp, dst[:, :, c], ALU.subtract)), 1
                    else:
                        n = did(pool.tensor_tensor(dst[:, :, c], dst[:, :, c], tmp, ALU.add if s_i == s else ALU.subtract))
                assert s > 0
                return n

            tile_rows = lambda b: b[:, 0:N].rearrange("p (t d) -> p t d", d=D)
            pool.wait_ge(a_act, AA_V + 7)
            n = did(pool.tensor_tensor(tile_rows(t2), tile_rows(t2), row[:, R_BKV + D:R_BKV + 2 * D].unsqueeze(1).broadcast_to([P, NT, D]), ALU.add))
            assert n == AP_V, n
            pool.wait_ge(a_dve, AD_KN)
            n = quat_component(quats(u), quats(t2), quats(t1), 3, False)
            assert n == AP_Q1, n
            pool.wait_ge(a_act, AA_MEM + 3)
            n = quat_component(quats(sq), quats(t2), quats(t1), 3, True)
            assert n == AP_Q2, n

            pool.wait_ge(in_tab, 32)
            def first_tiles(L):
                pool.wait_ge(w_high, L + 1)
                pool.tensor_tensor(wlo[:, :], wland, whi[:, :], ALU.subtract).then_inc(w_low, 1)
                pool.wait_ge(w_low, L + 1)
                pool.tensor_tensor(tabl[:, :, :], tab[:, :, :],
                                   scl[:, bass.ds(L, 1), :].broadcast_to([P, NT, 4 * DH]), ALU.mult).then_inc(tabs_ready, 1)
                finish_qk(L * NT)
                finish_qk(L * NT + 1)

            first_tiles(0)
            with pool.Fori(0, LAYERS - 1) as L:
                with pool.Fori(2, NT) as t:
                    finish_qk(L * NT + t)
                first_tiles(L + 1)
            with pool.Fori(2, NT) as t:
                finish_qk((LAYERS - 1) * NT + t)

        @block.scalar
        def _(act):
            step = [0]

            def did(ins, sem_=a_act):
                step[0] += 1
                ins.then_inc(sem_, 1)
                return step[0]

            def weights_high(L):
                act.wait_ge(in_wqkv, L * 16 + 16)
                act.wait_ge(qk_projected, L * (4 * NT) + FREE)
                act.wait_ge(v_projected, L * (2 * NT) + FREE)
                act.activation(whi[:, :], wland, ACT.Copy).then_inc(w_high, 1)

            act.wait_ge(in_vec, 48)
            assert did(act.activation(st[:, 1:2], vec[:, V_C:V_C + 1], ACT.Exp, scale=-1.0)) == AA_EXPC
            group = lambda b: slice(b * 512, b * 512 + 512)
            for b in range(4):
                act.wait_ge(a_dve, AD_XC1 + b)
                n = did(act.activation(t2[:, group(b)], t1[:, group(b)], ACT.Square))
                assert n == AA_SQ1 + b, n
            act.wait_ge(a_dve, AD_MOD)
            for b in range(4):
                act.wait_ge(a_pe, A_T1 + b)
                n = did(act.activation(hT[:, group(b)], ps[:, 4 + b, :], ACT.Identity, bias=vec[:, V_SA:V_SA + 1], scale=vec[:, V_CA:V_CA + 1]))
                assert n == AA_HT + b, n
            for b in range(4):
                act.wait_ge(a_dve, AD_K + b)
                did(act.activation(sq[:, group(b)], t1[:, group(b)], ACT.Square))
                n = did(act.activation(tok(t2)[:, 4 * b:4 * b + 4, :], kv_bank(b)[:, :, D:2 * D], ACT.Copy))
                assert n == AA_V + 2 * b + 1, n
            weights_high(0)
            act.wait_ge(a_dve, AD_Q1)
            act.wait_ge(a_pool, AP_Q1)
            for b in range(4):
                act.wait_ge(a_pe, A_CUM + b)
                for t in range(4 * b, 4 * b + 4):
                    ins = act.activation(tok(t2)[:, t, :], ps[:, b, (t % 4) * P:(t % 4) * P + P], ACT.Copy, scale=cst[:, C_RSQ + t:C_RSQ + t + 1])
                n = did(ins)
                assert n == AA_MEM + b, n
            for b in range(4):
                act.wait_ge(a_dve, AD_XC2 + b)
                n = did(act.activation(t2[:, group(b)], u[:, group(b)], ACT.Square))
                assert n == AA_SQ2 + b, n
            for b in range(4):
                act.wait_ge(a_pe, A_T2 + b)
                n = did(act.activation(t1[:, group(b)], ps[:, 4 + b, :], ACT.Identity, bias=vec[:, V_B:V_B + 1], scale=vec[:, V_G:V_G + 1]))
                assert n == AA_NT + b, n
            for b in range(4):
                act.wait_ge(a_dve, AD_XC3 + b)
                n = did(act.activation(t2[:, group(b)], t1[:, group(b)], ACT.Square))
                assert n == AA_SQ3 + b, n
            act.wait_ge(cleared, 3)
            for b in range(4):
                act.wait_ge(a_pe, A_T3 + b)
                n = did(act.activation(xT[:, 1 + b * 512:513 + b * 512], ps[:, 4 + b, :], ACT.Identity, bias=vec[:, V_SB:V_SB + 1], scale=vec[:, V_CB:V_CB + 1]))
                assert n == A_XT + b, n

            def evac_v(g, parities=range(2)):
                if 0 in parities:
                    act.wait_ge(v_stored, g * 16 + FREE)
                for a in parities:
                    act.wait_ge(v_projected, g * 2 + a + 1 + FREE)
                    act.activation(vs[:, a, :], ps[:, V_BANK[a], :], ACT.Copy).then_inc(v_evac, 1)

            def squares(g, chunks):
                if 0 in chunks:
                    act.wait_ge(sq_summed, g + FREE)
                for c in chunks:
                    act.wait_ge(qk_projected, g * 4 + c + 1 + FREE)
                    act.activation(sq[:, c * 512:c * 512 + 512], ps[:, QK_BANK[c], :], ACT.Square).then_inc(squared, 1)

            def probabilities(g):
                act.wait_ge(shifted, g + 1 + FREE)
                act.activation(pr[:, :, :], pr[:, :, :], ACT.Exp, scale=8.0).then_inc(exp_done, 1)

            def evac_p(g, banks=range(2)):
                if 0 in banks:
                    act.wait_ge(av_done, g * 2 + FREE)
                for b in banks:
                    act.wait_ge(p_trans, g * 2 + b + 1 + FREE)
                    act.activation(pT[:, 4 * b:4 * b + 4, :], bank(2 + b), ACT.Copy).then_inc(p_evac, 1)

            def evac_q(g):
                act.wait_ge(scored, g * 2 + FREE)
                act.activation(kT[:, :, :, 0:W], kT[:, :, :, P:P + W], ACT.Copy, scale=cst[:, C_KS:C_KS + 1]).then_inc(k_carried, 1)
                for b in range(2):
                    act.wait_ge(q_trans, g * 2 + b + 1)
                    act.activation(qT[:, 4 * b:4 * b + 4, :], bank(2 + b), ACT.Copy).then_inc(q_evac, 1)

            def evac_k(g, b):
                act.wait_ge(k_carried, g + 1)
                act.wait_ge(k_trans, g * 2 + b + 1 + FREE)
                for a in range(2):
                    r = slice(DH * a, DH * a + DH)
                    act.activation(kT[r, a, 4 * b:4 * b + 4, W:W + P], bank(b)[r], ACT.Copy).then_inc(k_evac, 1)

            def evac_o(g):
                act.wait_ge(y_done, g + FREE)
                for b in range(2):
                    act.wait_ge(o_trans, g * 2 + b + 1 + FREE)
                    act.activation(oT[:, 4 * b:4 * b + 4, :], bank(6 + b), ACT.Copy).then_inc(o_evac, 1)

            def bank(b):
                return ps[:, b, :].rearrange("p (a n) -> p a n", n=P)

            def shift(L, c):
                act.wait_ge(sq_summed, L * NT + NT + FREE)
                act.wait_ge(x_added, L * NT + (c + 1) * (CH // P) + FREE)
                act.activation(fxs[0:64, c, :], xT[0:64, 1 + c * CH:1 + c * CH + CH], ACT.Copy).then_inc(f_xs, 1)
                act.activation(fxs[64:P, c, :], xT[64:P, c * CH:c * CH + CH], ACT.Copy).then_inc(f_xs, 1)

            def centred(L, c):
                act.wait_ge(f_cen, L * NC_ + c + 1)
                act.wait_ge(f_prm, L + 1)
                act.wait_ge(added, (L * NT + NT) * 4 + FREE)
                act.activation(fxn[:, c, :], ps[:, CENTRE_BANK[c], :], ACT.Copy, scale=pl[:, L_G:L_G + 1]).then_inc(f_cp, 1)
                act.activation(fsq[:, c, :], ps[:, CENTRE_BANK[c], :], ACT.Square).then_inc(f_sq, 1)

            def gates(L, c, ks=range(3)):
                if 0 in ks:
                    act.wait_ge(f_bias, L * 2 + 2)
                    act.wait_ge(f_ag, L * (3 * NC_) + 3 * c + FREE)
                    act.wait_ge(f_y, L * NC_ + c + FREE)
                for k in ks:
                    act.wait_ge(f_gate, L * (3 * NC_) + 3 * c + k + 1)
                    act.activation(fg[0:KT[k], k, :], ps[0:KT[k], GATE_BANK(c, k), :], ACT.Gelu,
                                   bias=b1[0:KT[k], 1, k:k + 1]).then_inc(f_gelu, 1)

            def layer(L, more):
                with act.Fori(0, NT - 2) as t:
                    g = L * NT + t
                    squares(g + 2, (0, 1))
                    evac_v(g + 2, (0,))
                    probabilities(g)
                    evac_v(g + 2, (1,))
                    squares(g + 2, (2,))
                    evac_p(g)
                    squares(g + 2, (3,))
                    evac_q(g + 1)
                    evac_o(g)
                    evac_k(g + 1, 0)
                    evac_k(g + 1, 1)
                g = L * NT + NT - 1
                for c in range(NC_ - 1):
                    shift(L, c)
                centred(L, 0)
                probabilities(g - 1)
                centred(L, 1)
                evac_p(g - 1)
                centred(L, 2)
                evac_q(g)
                evac_o(g - 1)
                evac_k(g, 0)
                evac_k(g, 1)
                if more:
                    weights_high(L + 1)
                probabilities(g)
                evac_p(g)
                gates(L, 0, (0, 1))
                evac_o(g)
                gates(L, 0, (2,))
                centred(L, 3)
                n = (L + 1) * NT
                gates(L, 1)
                if more:
                    squares(n, range(4))
                    evac_v(n)
                gates(L, 2)
                if more:
                    squares(n + 1, range(4))
                    evac_v(n + 1)
                gates(L, 3)
                if more:
                    evac_q(n)
                    evac_k(n, 0)
                    evac_k(n, 1)

            for t in range(2):
                squares(t, range(4))
                evac_v(t)
            evac_q(0)
            evac_k(0, 0)
            evac_k(0, 1)
            with act.Fori(0, LAYERS - 1) as L:
                layer(L, True)
            layer(LAYERS - 1, False)

        @block.tensor
        def _(pe):
            step = [0]

            def did(ins):
                step[0] += 1
                ins.then_inc(a_pe, 1)
                return step[0]

            def tile(b, t):
                return ps[:, b + t // 4, (t % 4) * P:(t % 4) * P + P]

            pe.wait_ge(a_dve, AD_SILU)
            for j, m in enumerate((2, 5)):
                pe.matmul(ps[:, 6, P * j:P * j + P], st2[:, 0:P], wo[:, m, :], start=True, stop=True)
            for j, m in enumerate(MOD_ORDER):
                mm = pe.matmul(ps[:, 7, j:j + 1], wo[:, m, :], st[:, 4:5], start=True, stop=True)
            assert did(mm) == A_MOD

            def transpose_groups(src, ready, first):
                for t in range(NT):
                    if t % 4 == 0:
                        pe.wait_ge(a_dve, ready + t // 4)
                    mm = pe.transpose(tile(4, t), tok(src)[:, t, :], ident)
                    if t % 4 == 3:
                        n = did(mm)
                        assert n == first + t // 4, n

            transpose_groups(t1, AD_N1, A_T1)
            pe.wait_ge(in_wa, 32)
            for t in range(NT):
                if t % 4 == 0:
                    pe.wait_ge(a_act, AA_HT + t // 4)
                if t == 8:
                    pe.wait_ge(a_act, AA_HT + 3)
                mm = pe.matmul(ps[:, t // 2, (t % 2) * 256:(t % 2) * 256 + 256], hT[:, t * P:t * P + P], w1[:, 0:256], start=True, stop=True)
                if t % 4 == 3:
                    n = did(mm)
                    assert n == A_KV + t // 4, n
            pe.wait_ge(a_dve, AD_Q1)
            pe.wait_ge(a_pool, AP_Q1)
            for b in range(4):
                pe.matmul(ps[:, b, :], cst[:, C_TRI:C_TRI + P], u[:, b * 512:b * 512 + 512], start=True, stop=True)
                pe.wait_ge(a_dve, AD_PRE + 4 * b + 2)
                for t in range(max(1, 4 * b), 4 * b + 4):
                    mm = pe.matmul(tile(0, t), cst[:, C_ONE:C_ONE + P], pre[:, t, :], start=False, stop=True, skip_group_check=True)
                n = did(mm)
                assert n == A_CUM + b, n
            pe.wait_ge(a_act, AA_MEM + 3)
            for t in range(NT):
                if t % 4 == 0:
                    pe.matmul(ps[:, t // 4, :], cst[0:1, C_ONE:C_ONE + P], row[0:1, R_BO:R_BO + D].unsqueeze(1).broadcast_to([1, 4, D]),
                              start=True, stop=True)
                pe.matmul(tile(0, t), hT[:, t * P:t * P + P], ident, start=False, stop=True, skip_group_check=True)
            transpose_groups(u, AD_N2, A_T2)
            for t in range(NT):
                if t % 4 == 0:
                    pe.wait_ge(a_act, AA_NT + t // 4)
                mm = pe.matmul(tile(0, t), t1[:, t * P:t * P + P], w1[:, 256:384], start=False, stop=True, skip_group_check=True)
                if t % 4 == 3:
                    n = did(mm)
                    assert n == A_WO + t // 4, n
            transpose_groups(t1, AD_N3, A_T3)

            def project(g, before, chunks, ffn_x):
                if 0 in chunks:
                    pe.wait_ge(xs_ready, g * 4 + 4)
                    pe.wait_ge(rotated, g * 4 + FREE)
                for c in chunks:
                    if c == 0:
                        pe.wait_ge(o_normed, before * 2 + FREE)
                    if c == 4:
                        pe.wait_ge(x_added, before + FREE)
                        pe.wait_ge(v_evac, g * 2 + FREE)
                    if c == 5:
                        pe.wait_ge(f_x, ffn_x + FREE)
                    cols = slice(c * 512, c * 512 + 512)
                    for i, (x, w) in enumerate(((0, wlo), (1, whi), (0, whi))):
                        mm = pe.matmul(ps[:, (QK_BANK + V_BANK)[c], :], xs[:, x, :], w[:, cols], start=(i == 0), stop=(i == 2))
                    mm.then_inc(qk_projected if c < 4 else v_projected, 1)

            def transpose4(bk, src, b, done):
                for j in range(4):
                    mm = pe.transpose(ps[:, bk, j * P:j * P + P], src[:, (4 * b + j) * P:(4 * b + j + 1) * P], ident)
                mm.then_inc(done, 1)

            def transpose_q(g, projected):
                pe.wait_ge(q_normed, g + 1)
                pe.wait_ge(v_evac, projected * 2 + FREE)
                for b in range(2):
                    transpose4(2 + b, u[:, 0:INNER], b, q_trans)

            def transpose_k(g, projected, b):
                pe.wait_ge(k_normed, g + 1 + FREE)
                pe.wait_ge(rotated, projected * 4 - 1 + b + FREE)
                transpose4(b, u[:, INNER:2 * INNER], b, k_trans)

            def masks(g, m):
                pe.wait_ge(shifted, g + FREE)
                for b in range(2):
                    pe.matmul(ps[:, 4 + b, :], identb[:, :], maskb[:, m, :, :].rearrange("p h n -> p (h n)"), start=True, stop=True)

            def scores(g):
                pe.wait_ge(q_evac, g * 2 + 2)
                for b in range(2):
                    pe.wait_ge(k_evac, g * 4 + 2 * b + 2)
                    for j in range(4):
                        hp = 4 * b + j
                        for w in range(NW):
                            mm = pe.matmul(ps[W * w:W * w + W, 4 + b, j * P:j * P + P], qT[:, hp, W * w:W * w + W],
                                             kT[:, :, hp, W * w:W * w + 2 * W], start=False, stop=True,
                                             skip_group_check=True)
                    mm.then_inc(scored, 1)

            def transpose_p(g, projected):
                pe.wait_ge(exp_done, g + 1)
                pf = pr[:, :, :].rearrange("p h n -> p (h n)")
                for b in range(2):
                    pe.wait_ge(v_evac, projected * 2 - 1 + b + FREE)
                    transpose4(2 + b, pf, b, p_trans)

            def values(g, projected):
                pe.wait_ge(v_frames, g * 64 + 64 + FREE)
                pe.wait_ge(o_normed, g * 2 + FREE)
                for b in range(2):
                    pe.wait_ge(rotated, projected * 4 - 3 + b + FREE)
                    pe.wait_ge(p_evac, g * 2 + 1 + b)
                    for j in range(4):
                        hp = 4 * b + j
                        for w in range(NW):
                            mm = pe.matmul(ps[W * w:W * w + W, 6 + b, j * P:j * P + P],
                                             pT[:, hp, W * w:W * w + W], vf[:, :, w, hp * DH:hp * DH + DH],
                                             start=True, stop=True)
                    mm.then_inc(av_done, 1)

            def transpose_o(g):
                for b in range(2):
                    pe.wait_ge(o_normed, g * 2 + 1 + b + FREE)
                    transpose4(6 + b, o, b, o_trans)

            def project_o(g, transposed):
                pe.wait_ge(q_evac, transposed * 2 - 1)
                for k in range(HP):
                    pe.wait_ge(o_evac, g * 2 + 1 + k // 4)
                    mm = pe.matmul(ps[:, 2, 0:P], wo[:, k, :], oT[:, k, :], start=(k == 0), stop=(k == HP - 1))
                mm.then_inc(y_done, 1)

            def centre(L, c):
                f = L * NC_ + c
                pe.wait_ge(f_xs, f * 2 + 2)
                pe.matmul(ps[:, CENTRE_BANK[c], :], cen, fxs[:, c, :], start=True, stop=True).then_inc(f_cen, 1)

            def variances(L, part):
                lo, hi = PARTS[part]
                last = L * NC_ + hi * P // CH
                pe.wait_ge(f_cp, last)
                pe.wait_ge(f_sq, last)
                for t in range(lo, hi):
                    mm = pe.matmul(ps[:, VAR_BANK[part], t:t + P], t1[:, t * P:t * P + P], avg, start=True, stop=True)
                mm.then_inc(f_var, 1)

            def bias(L):
                pe.wait_ge(in_w12, L * 32 + 32)
                pe.wait_ge(f_prm, L + 1)
                for h in range(2):
                    for k in range(3):
                        i, c0 = 3 * h + k, DI * h + P * k
                        mm = pe.matmul(ps[0:KT[k], BIAS_BANK, i:i + 1], w1[:, c0:c0 + KT[k]], pl[:, L_B:L_B + 1], start=True, stop=True)
                mm.then_inc(f_bsum, 1)

            def std_rows(L, part):
                lo, hi = PARTS[part]
                pe.wait_ge(f_std, L * 2 + part + 1)
                pe.transpose(ps[0:hi - lo, ROW_BANK[part], STAT_ROW:STAT_ROW + P], frs[:, lo:hi], ident).then_inc(f_rows, 1)

            def std_everywhere(L, c):
                part = int(c == NC_ - 1)
                lo, hi = PARTS[part]
                pe.wait_ge(f_rowcopy, L * 2 + part + 1)
                if c == 2:
                    pe.wait_ge(f_xn, L * NC_ + 1)
                for j in range(CH // P):
                    t = 4 * c + j - lo
                    mm = pe.matmul(ps[:, STD_BANK[c], j * P:j * P + P], ident[0:hi - lo, t:t + 1].broadcast_to([hi - lo, P]),
                                   frow[0:hi - lo, part, :], start=True, stop=True)
                mm.then_inc(f_bc, 1)

            def gate_and_a(L, c, ks=range(3)):
                f = L * NC_ + c
                if 0 in ks:
                    pe.wait_ge(f_xn, f + 1)
                for k in ks:
                    i = L * (3 * NC_) + 3 * c + k - int(c == 0 and k > 0)
                    pe.wait_ge(f_gelu, i + FREE)
                    pe.matmul(ps[0:KT[k], GATE_BANK(c, k), :], w1[:, DI + P * k:DI + P * k + KT[k]], fxn[:, c, :],
                              start=True, stop=True).then_inc(f_gate, 1)
                    pe.wait_ge(f_ag, i + FREE)
                    pe.matmul(ps[0:KT[k], A_BANK(c, k), :], w1[:, P * k:P * k + KT[k]], fxn[:, c, :],
                              start=True, stop=True).then_inc(f_a, 1)

            def ffn_out(L, c):
                pe.wait_ge(f_x, L * NC_ + c + FREE)
                for k in range(3):
                    pe.wait_ge(f_ag, L * (3 * NC_) + 3 * c + k + 1 + FREE)
                    mm = pe.matmul(ps[:, Y_BANK, :], w2[0:KT[k], k, :], fg[0:KT[k], k, :], start=(k == 0), stop=(k == 2))
                mm.then_inc(f_y, 1)

            def back(L, b):
                pe.wait_ge(f_x, L * NC_ + b + 1 + FREE)
                for j in range(4):
                    mm = pe.transpose(ps[:, BACK_BANK[b], j * P:j * P + P], xT[:, 1 + (4 * b + j) * P:1 + (4 * b + j + 1) * P], ident)
                n = did(mm)
                assert n == C_T + b, n

            def layer(L, more):
                with pe.Fori(0, NT - 2) as t:
                    g = L * NT + t
                    project(g + 2, g, (0, 1, 4, 5, 2, 3), L * NC_)
                    transpose_p(g, g + 3)
                    masks(g + 1, 0)
                    values(g, g + 3)
                    transpose_q(g + 1, g + 3)
                    transpose_o(g)
                    transpose_k(g + 1, g + 3, 0)
                    transpose_k(g + 1, g + 3, 1)
                    project_o(g, g + 2)
                    scores(g + 1)
                end = L * NT + NT
                g = L * NT + NT - 1
                centre(L, 0)
                centre(L, 1)
                bias(L)
                centre(L, 2)
                pe.wait_ge(x_added, g - 1 + FREE)
                transpose_p(g - 1, end)
                masks(g, 0)
                pe.wait_ge(f_cp, L * NC_ + 2)
                pe.wait_ge(f_sq, L * NC_ + 2)
                values(g - 1, end)
                pe.wait_ge(f_bias, L * 2 + 2)
                variances(L, 0)
                pe.wait_ge(f_link, L * (2 * NORM_LINKS - 2) + 1)
                transpose_q(g, end)
                transpose_o(g - 1)
                transpose_k(g, end, 0)
                transpose_k(g, end, 1)
                pe.wait_ge(q_evac, end * 2)
                std_rows(L, 0)
                project_o(g - 1, end)
                std_everywhere(L, 0)
                scores(g)
                std_everywhere(L, 1)
                gate_and_a(L, 0, (0,))
                std_everywhere(L, 2)
                pe.wait_ge(x_added, g + FREE)
                transpose_p(g, end)
                pe.wait_ge(f_xn, L * NC_ + 3)
                values(g, end)
                gate_and_a(L, 0, (1,))
                transpose_o(g)
                gate_and_a(L, 0, (2,))
                project_o(g, end)
                n = (L + 1) * NT
                ffn_out(L, 0)
                centre(L, NC_ - 1)
                gate_and_a(L, 1, (0,))
                variances(L, 1)
                gate_and_a(L, 1, (1, 2))
                if more:
                    pe.wait_ge(w_low, L + 2)
                    project(n, n, (0, 1), 0)
                std_rows(L, 1)
                if more:
                    project(n, n, (2, 3), 0)
                std_everywhere(L, NC_ - 1)
                ffn_out(L, 1)
                if more:
                    pe.wait_ge(f_xn, L * NC_ + NC_)
                    project(n, n, (4, 5), L * NC_ + 2)
                gate_and_a(L, 2)
                if not more:
                    back(L, 0)
                if more:
                    project(n + 1, n, range(4), 0)
                    pe.wait_ge(v_evac, n * 2 + 2 + FREE)
                ffn_out(L, 2)
                if more:
                    project(n + 1, n, (4, 5), L * NC_ + 3)
                gate_and_a(L, 3)
                if not more:
                    back(L, 1)
                if more:
                    transpose_q(n, n + 2)
                    transpose_k(n, n + 2, 0)
                    transpose_k(n, n + 2, 1)
                    pe.wait_ge(q_evac, n * 2 + 2)
                ffn_out(L, 3)
                if not more:
                    back(L, 2)
                    back(L, 3)
                if more:
                    pe.wait_ge(in_wo, L * 16 + 32)
                    masks(n, 1)
                    scores(n)

            pe.wait_ge(masks_ready, 3)
            pe.wait_ge(w_low, 1)
            pe.wait_ge(in_wo, 16)
            pe.wait_ge(a_act, A_XT + 3)
            project(0, 0, range(6), 0)
            project(1, 0, range(6), 0)
            transpose_q(0, 2)
            transpose_k(0, 2, 0)
            transpose_k(0, 2, 1)
            masks(0, 1)
            scores(0)
            with pe.Fori(0, LAYERS - 1) as L:
                layer(L, True)
            layer(LAYERS - 1, False)

        @block.vector
        def _(v):
            step = [0]

            def did(ins):
                step[0] += 1
                ins.then_inc(a_dve, 1)
                v.wait_ge(a_dve, step[0])
                return step[0]

            def rsqrt(y, s, a):
                yield lambda: v.tensor_scalar(a.bitcast(I32), s.bitcast(I32), 1, None, ALU.arith_shift_right)
                yield lambda: v.tensor_scalar(y.bitcast(I32), a.bitcast(I32), -1.0, float(RSQRT_MAGIC), ALU.mult, ALU.add)
                for _ in range(NEWTON):
                    yield lambda: v.scalar_tensor_tensor(a, y, -0.5, y, ALU.mult, ALU.mult)
                    yield lambda: v.tensor_tensor(a, a, s, ALU.mult)
                    yield lambda: v.scalar_tensor_tensor(y, a, 1.5, y, ALU.add, ALU.mult)

            def centre(dst, src, mean):
                did(v.tensor_reduce(mean, src, AX, ALU.add))
                return subtract_mean(dst, src, mean)

            def subtract_mean(dst, src, mean):
                did(v.tensor_scalar(mean, mean, -1.0 / D, None, ALU.mult))
                for b in range(4):
                    n = did(v.tensor_tensor(tiles(dst, b), tiles(src, b), mean[:, 4 * b:4 * b + 4].unsqueeze(2).broadcast_to([P, 4, D]), ALU.add))
                return n - 3

            def normalise(dst, src, square, squared_step):
                for b in range(4):
                    v.wait_ge(a_act, squared_step + b)
                    did(v.tensor_reduce(st[:, 4 * b:4 * b + 4], tiles(square, b), AX, ALU.add))
                did(v.tensor_scalar(st[:, 0:NT], st[:, 0:NT], 1.0 / D, LN_EPS, ALU.mult, ALU.add))
                for newton in rsqrt(st2[:, 0:NT], st[:, 0:NT], st3[:, 0:NT]):
                    did(newton())
                for b in range(4):
                    n = did(v.tensor_tensor(tiles(dst, b), tiles(src, b), st2[:, 4 * b:4 * b + 4].unsqueeze(2).broadcast_to([P, 4, D]), ALU.mult))
                return n - 3

            def tiles(x, b):
                return x[:, 4 * b:4 * b + 4, :]

            def quat_components(dst, a, b, conj):
                tmps, cs = (st[:, :], st2[:, :], st3[:, :]), range(3)

                def turn(ins):
                    step[0] += 1
                    ins.then_inc(a_dve, 1)
                    v.wait_ge(a_dve, step[0] - 2)

                for c in cs:
                    s, k = quat_terms(0, c, conj)
                    turn(v.scalar_tensor_tensor(dst[:, :, c], a[:, :, 0], float(s), b[:, :, k], ALU.mult, ALU.mult))
                for i in range(1, 4):
                    for c in cs:
                        turn(v.tensor_tensor(tmps[c], a[:, :, i], b[:, :, quat_terms(i, c, conj)[1]], ALU.mult))
                    for c in cs:
                        turn(v.tensor_tensor(dst[:, :, c], dst[:, :, c], tmps[c], ALU.add if quat_terms(i, c, conj)[0] > 0 else ALU.subtract))
                v.wait_ge(a_dve, step[0])
                return step[0]

            v.wait_ge(in_x, 16)
            mean = st[:, 8:8 + NT]
            did(v.tensor_reduce(mean, x1[:, :, :], AX, ALU.add))
            v.wait_ge(a_act, AA_EXPC)
            did(v.tensor_scalar(st[:, 2:3], st[:, 1:2], 1.0, None, ALU.add))
            did(v.reciprocal(st[:, 3:4], st[:, 2:3]))
            did(v.tensor_tensor(st[:, 4:5], st[:, 3:4], vec[:, V_C:V_C + 1], ALU.mult))
            v.wait_ge(in_cst, 16)
            n = did(v.tensor_scalar(st2[:, 0:P], cst[:, C_ONE:C_ONE + P], st[:, 4:5], None, ALU.mult))
            assert n == AD_SILU, n
            n = subtract_mean(tok(t1), x1[:, :, :], mean)
            assert n == AD_XC1, n
            ga, gb = mod[:, 0:D], mod[:, D:2 * D]
            v.wait_ge(a_pe, A_MOD)
            did(v.tensor_copy(vec[:, V_SA:V_CB + 1], ps[:, 7, 0:4]))
            for c in (V_CA, V_CB):
                did(v.tensor_scalar(vec[:, c:c + 1], vec[:, c:c + 1], 1.0, None, ALU.add))
            did(v.tensor_copy(mod[:, :], ps[:, 6, 0:2 * D]))
            m, sign, size = mod[:, :], st3[:, 0:2 * D], fg[:, 1, 0:2 * D]
            did(v.tensor_scalar(sign, m, 0.0, None, ALU.is_ge))
            did(v.tensor_scalar(sign, sign, 2.0, -1.0, ALU.mult, ALU.add))
            did(v.tensor_scalar(size, m, -1.0, 0.25, ALU.mult, ALU.max))
            did(v.tensor_tensor(m, m, size, ALU.max))
            n = did(v.tensor_tensor(m, m, sign, ALU.mult))
            assert n == AD_MOD, n
            n = normalise(tok(t1), tok(t1), tok(t2), AA_SQ1)
            assert n == AD_N1, n
            for b in range(4):
                v.wait_ge(a_pe, A_KV + b)
                n = did(v.tensor_tensor(tok(t1)[:, 4 * b:4 * b + 4, :], kv_bank(b)[:, :, 0:D],
                                        row[:, R_BKV:R_BKV + D].unsqueeze(1).broadcast_to([P, 4, D]), ALU.add))
                assert n == AD_K + b, n
            v.wait_ge(a_act, AA_V + 6)
            did(v.tensor_reduce(st[:, :], quats(sq), AX, ALU.add))
            did(v.tensor_scalar(st[:, :], st[:, :], NORM_GUARD, None, ALU.max))
            for newton in rsqrt(st2[:, :], st[:, :], st3[:, :]):
                did(newton())
            n = did(v.tensor_tensor(quats(t1), quats(t1), st2[:, :].unsqueeze(2).broadcast_to([P, NQ, 4]), ALU.mult))
            assert n == AD_KN, n
            v.wait_ge(a_pool, AP_V)
            n = quat_components(quats(u), quats(t2), quats(t1), False)
            assert n == AD_Q1, n
            v.wait_ge(a_pool, AP_Q1)
            n = did(v.tensor_copy(pre[:, 1, :], tok(u)[:, 0, :]))
            for t in range(2, NT):
                n = did(v.tensor_tensor(pre[:, t, :], pre[:, t - 1, :], tok(u)[:, t - 1, :], ALU.add))
            assert n == AD_PRE + NT - 2, n
            v.wait_ge(a_act, AA_MEM + 3)
            n = quat_components(quats(sq), quats(t2), quats(t1), True)
            assert n == AD_Q2, n
            v.wait_ge(a_pool, AP_Q2)
            n = centre(tok(u), tok(sq), st[:, 0:NT])
            assert n == AD_XC2, n
            n = normalise(tok(u), tok(u), tok(t2), AA_SQ2)
            assert n == AD_N2, n
            for b in range(4):
                v.wait_ge(a_pe, A_WO + b)
                y = ps[:, b, :].rearrange("p (t d) -> p t d", d=D)
                did(v.tensor_tensor(tok(sq)[:, 4 * b:4 * b + 4, :], y, ga.unsqueeze(1).broadcast_to([P, 4, D]), ALU.mult))
                n = did(v.tensor_tensor(x1[:, 4 * b:4 * b + 4, :], x1[:, 4 * b:4 * b + 4, :], tok(sq)[:, 4 * b:4 * b + 4, :], ALU.add))
                assert n == AD_X1 + 2 * b + 1, n
            n = centre(tok(t1), x1[:, :, :], st[:, 0:NT])
            assert n == AD_XC3, n
            n = normalise(tok(t1), tok(t1), tok(t2), AA_SQ3)
            assert n == AD_N3, n

            def stage(t, g):
                v.wait_ge(v_projected, g * 2 + FREE)
                v.wait_ge(qk_projected, g * 4 + FREE)
                halves = ((slice(0, 64), xT[0:64, bass.ds(t * P + 1, P)]), (slice(64, P), xT[64:P, bass.ds(t * P, P)]))
                for r, x in halves:
                    v.tensor_scalar(xs[r, 0, :], x, 1.0, None, ALU.mult).then_inc(xs_ready, 1)
                for j, (r, x) in enumerate(halves):
                    v.wait_ge(xs_ready, g * 4 + j + 1)
                    v.tensor_tensor(xs[r, 1, :], x, xs[r, 0, :], ALU.subtract).then_inc(xs_ready, 1)

            def rotate(t, g, chunks=range(4)):
                v.wait_ge(added, g * 4 + FREE)
                for c in chunks:
                    v.wait_ge(squared, g * 4 + c + 1)
                    q = ps[:, QK_BANK[c], :].rearrange("p (h d) -> p h d", d=DH).unsqueeze(1).broadcast_to([P, 2, 8, DH])
                    j = 2 * (c // 2)
                    cs = tabl[:, bass.ds(t, 1), j * DH:(j + 2) * DH].rearrange("p a (s d) -> p s a d", d=DH).broadcast_to([P, 2, 8, DH])
                    v.tensor_tensor(tr[:, c, :, :].rearrange("p s (h d) -> p s h d", d=DH), q, cs, ALU.mult).then_inc(rotated, 1)

            def sum_squares(g):
                v.wait_ge(folded, g + 1)
                v.tensor_reduce(ss[:, :], sq[:, :].rearrange("p (h s d) -> p h s d", s=2, d=DH // 2)[:, :, 0, :], AX, ALU.add).then_inc(sq_summed, 1)

            def inv_norms(g, steps=range(NORM_LINKS)):
                if 0 in steps:
                    v.wait_ge(sq_summed, g + 1 + FREE)
                    v.wait_ge(k_normed, g + FREE)
                    v.tensor_scalar(ss[:, :], ss[:, :], NORM_GUARD, None, ALU.max).then_inc(link, 1)
                for n, newton in enumerate(rsqrt(rn[:, :], ss[:, :], ra[:, :])):
                    if n + 1 not in steps:
                        continue
                    v.wait_ge(link, g * NORM_LINKS + n + 1)
                    newton().then_inc(link, 1)

            def shift_by_max(g, newton=None):
                v.wait_ge(p_trans, g * 2 + FREE)
                s = ps[:, 4:6, :].rearrange("p b (h n) -> p (b h) n", n=2 * W)
                for b in range(2):
                    v.wait_ge(scored, g * 2 + b + 1 + FREE)
                    v.tensor_reduce(mx[:, 8 * b:8 * b + 8], s[:, 8 * b:8 * b + 8, :], AX, ALU.max).then_inc(max_ready, 1)
                    if newton is not None:
                        inv_norms(newton, range(EARLY + 2 * b, EARLY + 2 * b + 2))
                v.wait_ge(max_ready, g * 2 + 2)
                v.tensor_tensor(pr[:, :, :], s, mx[:, :].unsqueeze(2).broadcast_to([P, H, 2 * W]), ALU.subtract).then_inc(shifted, 1)

            def inv_sums(g):
                v.wait_ge(exp_done, g + 1)
                v.tensor_reduce(rs[:, :], pr[:, :, :], AX, ALU.add).then_inc(sum_ready, 1)
                v.wait_ge(sum_ready, g + 1)
                v.reciprocal(ri[:, :], rs[:, :]).then_inc(rsum_ready, 1)

            def output(g):
                v.wait_ge(rsum_ready, g + 1)
                v.wait_ge(o_trans, g * 2 + FREE)
                for b in range(2):
                    v.wait_ge(av_done, g * 2 + b + 1 + FREE)
                    v.tensor_tensor(o[:, 512 * b:512 * b + 512].rearrange("p (h n) -> p h n", n=DH),
                                    ps[:, 6 + b, :].rearrange("p (h n) -> p h n", n=DH),
                                    ri[:, 8 * b:8 * b + 8].unsqueeze(2).broadcast_to([P, 8, DH]), ALU.mult).then_inc(o_normed, 1)

            def add_x(t, g):
                v.wait_ge(y_done, g + 1 + FREE)
                xt = xT[:, bass.ds(t * P + 1, P)]
                v.tensor_tensor(xt, ps[:, 2, 0:P], xt, ALU.add).then_inc(x_added, 1)

            v.wait_ge(in_prm, 16)
            v.wait_ge(a_act, A_XT)
            def shift_last(L):
                c = NC_ - 1
                v.wait_ge(x_added, L * NT + NT + FREE)
                v.tensor_copy(fxs[0:64, c, :], xT[0:64, 1 + c * CH:1 + c * CH + CH]).then_inc(f_xs, 1)
                v.tensor_copy(fxs[64:P, c, :], xT[64:P, c * CH:c * CH + CH]).then_inc(f_xs, 1)

            def inv_deviations(L, part):
                lo, hi = PARTS[part]
                n = (L * 2 + part) * (NORM_LINKS - 1)
                v.wait_ge(f_var, L * 2 + part + 1)
                v.tensor_scalar(fvar[:, lo:hi], ps[:, VAR_BANK[part], lo:hi], 1.0, LN_EPS, ALU.mult, ALU.add).then_inc(f_link, 1)
                steps = list(rsqrt(frs[:, lo:hi], fvar[:, lo:hi], fra[:, lo:hi]))
                for i, newton in enumerate(steps):
                    v.wait_ge(f_link, n + i + 1)
                    ins = newton().then_inc(f_link if i + 1 < len(steps) else f_std, 1)

            def copy_rows(L, part):
                lo, hi = PARTS[part]
                v.wait_ge(f_rows, L * 2 + part + 1)
                v.tensor_copy(frow[0:hi - lo, part, :], ps[0:hi - lo, ROW_BANK[part], STAT_ROW:STAT_ROW + P]).then_inc(f_rowcopy, 1)

            def biases(L):
                v.wait_ge(f_bsum, L + 1)
                own, more = pl[:, L_BA:L_BA + 6].rearrange("p (h k) -> p h k", k=3), ps[:, BIAS_BANK, 0:6].rearrange("p (h k) -> p h k", k=3)
                v.tensor_tensor(b1[:, :, 0:2], own[:, :, 0:2], more[:, :, 0:2], ALU.add).then_inc(f_bias, 1)
                v.tensor_tensor(b1[0:KT[2], :, 2:3], own[0:KT[2], :, 2:3], more[0:KT[2], :, 2:3], ALU.add).then_inc(f_bias, 1)

            def normalise_chunk(L, c):
                f = L * NC_ + c
                v.wait_ge(f_bc, f + 1)
                v.wait_ge(f_cp, f + 1)
                v.tensor_tensor(fxn[:, c, :], ps[:, STD_BANK[c], :], fxn[:, c, :], ALU.mult).then_inc(f_xn, 1)

            def gated(L, c, ks=range(3)):
                v.wait_ge(f_bias, L * 2 + 2)
                for k in ks:
                    i = L * (3 * NC_) + 3 * c + k + 1
                    v.wait_ge(f_a, i)
                    v.wait_ge(f_gelu, i + FREE)
                    g_ = fg[0:KT[k], k, :]
                    v.scalar_tensor_tensor(g_, ps[0:KT[k], A_BANK(c, k), :], b1[0:KT[k], 0, k:k + 1], g_, ALU.add, ALU.mult).then_inc(f_ag, 1)

            def ffn_add_x(L, c):
                v.wait_ge(f_y, L * NC_ + c + 1 + FREE)
                xt = xT[:, 1 + c * CH:1 + c * CH + CH]
                v.scalar_tensor_tensor(xt, ps[:, Y_BANK, :], pl[:, L_B2:L_B2 + 1], xt, ALU.add, ALU.add).then_inc(f_x, 1)

            def finish(b):
                v.wait_ge(a_pe, C_T + b)
                y = ps[:, BACK_BANK[b], :].rearrange("p (t d) -> p t d", d=D)
                did(v.tensor_tensor(tiles(tok(u), b), y, gb.unsqueeze(1).broadcast_to([P, 4, D]), ALU.mult))
                n = did(v.tensor_tensor(tiles(x1, b), tiles(x1, b), tiles(tok(u), b), ALU.add))
                assert n == C_OUT + 2 * b, n

            def layer(L, more):
                v.wait_ge(f_x, L * NC_ + FREE)
                v.tensor_copy(pl[:, :], prm[:, bass.ds(L, 1), :].rearrange("p a n -> p (a n)")).then_inc(f_prm, 1)
                def step(t, g, more_tiles):
                    shift_by_max(g, g + 1)
                    rotate(t + 2, g + 2, (0, 1))
                    inv_sums(g)
                    rotate(t + 2, g + 2, (2,))
                    output(g)
                    rotate(t + 2, g + 2, (3,))
                    if more_tiles:
                        stage(t + 3, g + 3)
                    sum_squares(g + 2)
                    inv_norms(g + 2, range(5))
                    add_x(t, g)
                    inv_norms(g + 2, range(5, EARLY))

                with v.Fori(0, NT - 3) as t:
                    step(t, L * NT + t, True)
                step(NT - 3, L * NT + NT - 3, False)
                g = L * NT + NT - 1
                shift_by_max(g - 1, g)
                inv_sums(g - 1)
                v.wait_ge(f_prm, L + 1)
                biases(L)
                output(g - 1)
                inv_deviations(L, 0)
                copy_rows(L, 0)
                add_x(NT - 2, g - 1)
                normalise_chunk(L, 0)
                shift_by_max(g)
                normalise_chunk(L, 1)
                normalise_chunk(L, 2)
                inv_sums(g)
                gated(L, 0, (0,))
                output(g)
                gated(L, 0, (1, 2))
                add_x(NT - 1, g)
                shift_last(L)
                n = (L + 1) * NT
                ffn_add_x(L, 0)
                if more:
                    v.wait_ge(f_x, L * NC_ + 1 + FREE)
                    stage(0, n)
                    v.wait_ge(tabs_ready, L + 2)
                gated(L, 1, (0, 1))
                inv_deviations(L, 1)
                gated(L, 1, (2,))
                copy_rows(L, 1)
                if more:
                    rotate(0, n, (0, 1))
                normalise_chunk(L, 3)
                if more:
                    rotate(0, n, (2,))
                ffn_add_x(L, 1)
                if more:
                    rotate(0, n, (3,))
                if more:
                    stage(1, n + 1)
                gated(L, 2, (0, 1))
                if more:
                    sum_squares(n)
                    inv_norms(n, range(6))
                gated(L, 2, (2,))
                if more:
                    inv_norms(n, range(6, NORM_LINKS))
                if more:
                    rotate(1, n + 1, (0,))
                ffn_add_x(L, 2)
                if more:
                    rotate(1, n + 1, (1, 2, 3))
                if not more:
                    finish(0)
                gated(L, 3)
                if not more:
                    finish(1)
                if more:
                    stage(2, n + 2)
                    sum_squares(n + 1)
                    inv_norms(n + 1, range(EARLY))
                ffn_add_x(L, 3)
                if not more:
                    finish(2)
                    finish(3)

            stage(0, 0)
            v.wait_ge(tabs_ready, 1)
            rotate(0, 0)
            stage(1, 1)
            sum_squares(0)
            inv_norms(0)
            rotate(1, 1)
            stage(2, 2)
            sum_squares(1)
            inv_norms(1, range(EARLY))
            v.wait_ge(a_act, A_XT + 3)
            with v.Fori(0, LAYERS - 1) as L:
                layer(L, True)
            layer(LAYERS - 1, False)


def rotary_tables():
    f = np.float32
    half = np.arange(0, DH, 2, dtype=f)
    inv_freq = (f(1) / np.power(f(10000), half / f(DH))).astype(f)
    pos = np.arange(N, dtype=f)
    freqs = (pos[:, None] * inv_freq[None, :]).astype(f).astype(np.float64)
    base = ((half + f(0.4 * DH)) / f(1.4 * DH)).astype(np.float64)
    scale = base[None, :] ** ((np.arange(N) % P - P // 2) / (W // 2))[:, None]
    cos, sin = np.cos(freqs), np.sin(freqs)
    parts = []
    for s in (scale, 1.0 / scale):
        parts += [cos * s, cos * s, sin * s, -sin * s]
    carry = np.tile(base ** (P / (W // 2)), P // len(base))
    return np.concatenate(parts, 1).astype(f), carry.astype(f)


def constants(carry):
    c = np.zeros((P, C_END), np.float32)
    i = np.arange(P)
    c[:, C_ID:C_ID + P] = np.eye(P)
    c[:, C_TRI:C_TRI + P] = i[:, None] <= i[None, :]
    c[:, C_ONE:C_ONE + P] = 1
    c[:, C_AVG:C_AVG + P] = 1 / D
    c[:, C_CEN:C_CEN + P] = np.eye(P) - 1 / D
    q, k = i[:, None] % W, np.arange(2 * W)[None, :]
    seen = (k >= q) & (k <= q + W)
    c[:, C_MASK:C_MASK + 2 * W] = np.where(seen, 0, MASKED)
    c[:, C_MASK0:C_MASK0 + 2 * W] = np.where(seen & ((i[:, None] >= W) | (k >= W)), 0, MASKED)
    c[:, C_KS] = carry
    c[:, C_RSQ:C_RSQ + NT] = 1 / np.sqrt(np.arange(1, N + 1).reshape(NT, P).T)
    c[:, C_EPS] = LN_EPS
    return c


def kernel(**inputs):
    import concourse.bacc as bacc
    from concourse.bass_utils import run_bass_kernel_spmd

    a = {k: np.asarray(v) for k, v in inputs.items()}
    f = np.float32
    tab, carry = rotary_tables()
    wqkv = a["L0_ffn_Wqkv"]
    v = wqkv[:, :, 2 * INNER:].reshape(LAYERS, D, HP, 2, DH).transpose(0, 1, 3, 2, 4).reshape(LAYERS, D, INNER)
    qs, ks = a["L0_ffn_q_scale"], a["L0_ffn_k_scale"]
    w2 = np.zeros((LAYERS, 3 * P, D), f)
    w2[:, :DI] = a["L0_ffn_W2"]
    prm = np.zeros((P, LAYERS, L_END), f)
    prm[:, :, L_G], prm[:, :, L_B], prm[:, :, L_B2] = a["L0_ffn_ln_g"].T, a["L0_ffn_ln_b"].T, a["L0_ffn_b2"].T
    for k, n in enumerate(KT):
        prm[:n, :, L_BA + k] = a["L0_ffn_b1"][:, P * k:P * k + n].T
        prm[:n, :, L_BG + k] = a["L0_ffn_b1"][:, DI + P * k:DI + P * k + n].T
    arrays = {
        "x": a["L0_attn_x"][0],
        "cst": constants(carry),
        "row": np.concatenate([a["L0_attn_bk"], a["L0_attn_bv"], a["L0_attn_bo"]]),
        "c": np.stack([a["L0_c"].reshape(D), a["L0_attn_ln_g"], a["L0_attn_ln_b"]], 1),
        "wmod": a["L0_wmod"],
        "wkv": np.concatenate([a["L0_attn_Wk"].T, a["L0_attn_Wv"].T], 1),
        "woa": a["L0_attn_Wo"].T,
        "tab": tab,
        "scl": np.concatenate([qs, qs, ks, ks], 1),
        "wqkv": np.concatenate([wqkv[:, :, :2 * INNER], v], 2).reshape(LAYERS * D, 3 * INNER),
        "wo": a["L0_ffn_Wo"].reshape(LAYERS, HP, P, D).transpose(0, 2, 1, 3).reshape(LAYERS * P, HP * D),
        "w1": a["L0_ffn_W1"].reshape(LAYERS * D, 2 * DI),
        "w2": w2.reshape(LAYERS, 3, P, D).transpose(0, 2, 1, 3).reshape(LAYERS * P, 3 * D),
        "prm": prm,
    }
    arrays = {f"in_{k}": np.ascontiguousarray(x) for k, x in arrays.items()}
    nc = bacc.Bacc("TRN2", target_bir_lowering=False, num_devices=1)
    args = [nc.dram_tensor(k, x.shape, mybir.dt.from_np(x.dtype), kind="ExternalInput").ap() for k, x in arrays.items()]
    out = nc.dram_tensor("out", [N, D], F32, kind="ExternalOutput").ap()
    program(nc, *args, out)
    r = run_bass_kernel_spmd(nc, [arrays], core_ids=[0])
    return r.results[0]["out"].reshape(1, N, D)
```
